# Optimizing a Trainium2 kernel written in Bass

```python
import numpy as np
import jax
import jax.numpy as jnp

def _softmax(x, axis=-1):
    return jax.nn.softmax(x, axis=axis)

def _gelu(x):
    return jax.nn.gelu(x, approximate=True)

def _silu(x):
    return jax.nn.silu(x)

def _sigmoid(x):
    return jax.nn.sigmoid(x)

def _layernorm(x, axis=-1, eps=1e-05):
    m = jnp.mean(x, axis=axis, keepdims=True)
    v = jnp.var(x, axis=axis, keepdims=True)
    return (x - m) / jnp.sqrt(v + eps)

def _scatter_add(tgt, idx, src, axis=0):
    return tgt.at[idx].add(src)

def _segment_sum(src, seg, n):
    return jax.ops.segment_sum(src, seg, n)
kernel_name = 'mk_macaron_d1_jaxref_r4_4d23a0'

def setup_inputs(seed: int=0):
    np.random.seed(seed)
    _w = jnp.asarray

    def _L0_attn_setup():
        import jax, jax.numpy as jnp
        import numpy as np
        EPS = 1e-08
        key = jax.random.key(seed)
        k0, k1, k2, k3 = jax.random.split(key, 4)
        B, S, D = (8, 512, 256)
        scale = 1.0 / np.sqrt(D)
        x = jax.random.normal(k0, (B, S, D), dtype=jnp.float32)
        Wq = jax.random.normal(k1, (D, D), dtype=jnp.float32) * scale
        Wk = jax.random.normal(k2, (D, D), dtype=jnp.float32) * scale
        Wv = jax.random.normal(k3, (D, D), dtype=jnp.float32) * scale
        return {'x': x, 'Wq': Wq, 'Wk': Wk, 'Wv': Wv}
    _L0_attn_in = _L0_attn_setup()

    def _L0_ffn_setup():
        import jax, jax.numpy as jnp
        import numpy as np
        D_MODEL = 256
        H_SHARED = 512
        H_ROUTED = 256
        N_EXPERTS = 8
        TOP_K = 2
        key = jax.random.key(seed)
        ks = jax.random.split(key, 8)
        B, T = (2, 512)
        sc_d = 1.0 / np.sqrt(D_MODEL)
        sc_hs = 1.0 / np.sqrt(H_SHARED)
        sc_hr = 1.0 / np.sqrt(H_ROUTED)
        return {'x': jax.random.normal(ks[0], (B, T, D_MODEL), dtype=jnp.float32), 'router_w': jax.random.normal(ks[1], (N_EXPERTS, D_MODEL), dtype=jnp.float32) * sc_d, 'router_bias': jnp.zeros((N_EXPERTS,), dtype=jnp.float32), 'sw1': jax.random.normal(ks[2], (D_MODEL, H_SHARED), dtype=jnp.float32) * sc_d, 'sw3': jax.random.normal(ks[3], (D_MODEL, H_SHARED), dtype=jnp.float32) * sc_d, 'sw2': jax.random.normal(ks[4], (H_SHARED, D_MODEL), dtype=jnp.float32) * sc_hs, 'ew1': jax.random.normal(ks[5], (N_EXPERTS, D_MODEL, H_ROUTED), dtype=jnp.float32) * sc_d, 'ew2': jax.random.normal(ks[6], (N_EXPERTS, H_ROUTED, D_MODEL), dtype=jnp.float32) * sc_hr}
    _L0_ffn_in = _L0_ffn_setup()
    _d = {'L0_attn_x': _L0_attn_in['x'], 'L0_attn_Wq': _L0_attn_in['Wq'], 'L0_attn_Wk': _L0_attn_in['Wk'], 'L0_attn_Wv': _L0_attn_in['Wv'], 'L0_ffn_router_w': _L0_ffn_in['router_w'], 'L0_ffn_router_bias': _L0_ffn_in['router_bias'], 'L0_ffn_sw1': _L0_ffn_in['sw1'], 'L0_ffn_sw3': _L0_ffn_in['sw3'], 'L0_ffn_sw2': _L0_ffn_in['sw2'], 'L0_ffn_ew1': _L0_ffn_in['ew1'], 'L0_ffn_ew2': _L0_ffn_in['ew2']}
    _x0 = _d['L0_attn_x']
    _d['L0_attn_x'] = jax.random.normal(jax.random.fold_in(jax.random.key(seed), 1), (8, 1024, 256), dtype=_x0.dtype)
    del _x0
    return _d

def reference(L0_attn_x, L0_attn_Wq, L0_attn_Wk, L0_attn_Wv, L0_ffn_router_w, L0_ffn_router_bias, L0_ffn_sw1, L0_ffn_sw3, L0_ffn_sw2, L0_ffn_ew1, L0_ffn_ew2):

    def _L0_attn_ref(x, Wq, Wk, Wv):
        import jax, jax.numpy as jnp
        import numpy as np
        EPS = 1e-08
        D = x.shape[-1]
        q = jnp.einsum('bsd,ed->bse', x, Wq)
        k = jnp.einsum('bsd,ed->bse', x, Wk)
        v = jnp.einsum('bsd,ed->bse', x, Wv)
        fk = jnp.fft.rfft(k, axis=-1)
        fk = fk / (jnp.abs(fk) + EPS)
        fq = jnp.fft.rfft(q, axis=-1)
        fq = fq / (jnp.abs(fq) + EPS)
        fv = jnp.fft.rfft(v, axis=-1)
        fkv = jnp.cumsum(fk * fv, axis=-2)
        values_hat = jnp.fft.irfft(fkv * jnp.conj(fq), n=D, axis=-1)
        return x + values_hat

    def _L0_ffn_ref(x, router_w, router_bias, sw1, sw3, sw2, ew1, ew2):
        import jax, jax.numpy as jnp
        import numpy as np
        D_MODEL = 256
        H_SHARED = 512
        H_ROUTED = 256
        N_EXPERTS = 8
        TOP_K = 2
        B, T, C = x.shape
        xf = x.reshape(-1, C)
        shared_out = jax.nn.silu(xf @ sw1) * (xf @ sw3) @ sw2
        s = jax.nn.sigmoid((xf @ router_w.T).astype(jnp.float32))
        sel_scores = s + router_bias.astype(jnp.float32)
        _, topk_idx = jax.lax.top_k(sel_scores, TOP_K)
        s_sel = jnp.take_along_axis(s, topk_idx, axis=1)
        denom = s_sel.sum(axis=1, keepdims=True)
        gates = jnp.where(denom > 1e-09, s_sel / (denom + 1e-09), 1.0 / TOP_K).astype(x.dtype)
        one_hot = jax.nn.one_hot(topk_idx, N_EXPERTS, dtype=x.dtype)
        comb = jnp.einsum('nke,nk->ne', one_hot, gates)
        h = jax.nn.gelu(jnp.einsum('nd,edh->neh', xf, ew1), approximate=False)
        y = jnp.einsum('neh,ehd->ned', h, ew2)
        routed_out = jnp.einsum('ned,ne->nd', y, comb)
        return (shared_out + routed_out).reshape(B, T, C)
    x = L0_attn_x
    x = x + 0.5 * _L0_ffn_ref(_layernorm(x, axis=-1), L0_ffn_router_w, L0_ffn_router_bias, L0_ffn_sw1, L0_ffn_sw3, L0_ffn_sw2, L0_ffn_ew1, L0_ffn_ew2)
    x = x + _L0_attn_ref(_layernorm(x, axis=-1), L0_attn_Wq, L0_attn_Wk, L0_attn_Wv)
    x = x + 0.5 * _L0_ffn_ref(_layernorm(x, axis=-1), L0_ffn_router_w, L0_ffn_router_bias, L0_ffn_sw1, L0_ffn_sw3, L0_ffn_sw2, L0_ffn_ew1, L0_ffn_ew2)
    return x

_drawn_inputs = setup_inputs


def setup_inputs(seed=0):
    import zlib

    import numpy as np

    out = dict(_drawn_inputs(seed))
    spreads = {'L0_ffn_router_bias': (0.0, 0.1)}
    factors = {}
    for name, (base, spread) in spreads.items():
        noise = np.random.default_rng([zlib.crc32(name.encode()), seed]).standard_normal(out[name].shape)
        drawn = base * np.exp(spread * noise) if base else spread * noise
        out[name] = jnp.asarray(drawn.astype(out[name].dtype))
    for name, factor in factors.items():
        out[name] = (out[name] * factor).astype(out[name].dtype)
    return out
```

```python
from contextlib import ExitStack

import numpy as np

import concourse.bass as bass
from concourse import mybir

F32 = mybir.dt.float32
F32R = mybir.dt.float32r
BF16 = mybir.dt.bfloat16
I32 = mybir.dt.int32
ALU = mybir.AluOpType
ACT = mybir.ActivationFunctionType
AX = mybir.AxisListType

P = 128
B, S, D = 8, 1024, 256
TOKENS = B * S
TILES = TOKENS // P
J = 4
CH = TILES // J
N = J * P
KD = D // P
FS = 512
M = FS // P
E, TOPK = 8, 2
HR = 256
CAP = TOKENS + P
ROW = D + 8
BLOCKS = TOPK * TILES + E
PAIRS = BLOCKS // 2
LN_EPS, FFT_EPS, GATE_EPS = 1e-5, 1e-8, 1e-9
NF = D // 2
NW = D + 2

DVE_A, DVE_T = 86, 63

C_ID, C_TRI, C_ONE, C_RESE, C_RESJ = 0, 128, 256, 384, 416
C_BASE, C_ONE8, C_THR, C_BLK, C_END = 448, 456, 464, 528, 528 + BLOCKS


def constants():
    c = np.zeros((P, C_END), np.float32)
    p = np.arange(P)
    c[:, C_ID:C_ID + P] = np.eye(P)
    c[:, C_TRI:C_TRI + P] = p[:, None] <= p[None, :]
    c[:, C_ONE:C_ONE + P] = 1.0
    c[:, C_RESE:C_RESE + J * E] = (np.arange(J * E) % E != 0)
    c[:, C_RESJ:C_RESJ + J * E] = (np.arange(J * E) % J != 0)
    c[:, C_BASE:C_BASE + E] = np.arange(E) * CAP
    c[:, C_ONE8:C_ONE8 + E] = 1.0
    c[:, C_THR:C_THR + TILES] = np.arange(TILES) * P
    c[:, C_BLK:C_BLK + BLOCKS] = np.arange(BLOCKS)
    n = np.arange(D)[:, None].astype(np.float64)
    f = np.arange(NF)[None, :].astype(np.float64)
    ang = 2.0 * np.pi * n * f / D
    fwd = np.zeros((D, NW), np.float32)
    fwd[:, :NF] = np.cos(ang)
    fwd[:, NF:D] = -np.sin(ang)
    fwd[:, D] = 1.0 - 2.0 * (np.arange(D) % 2)
    w = np.full((NF, 1), 2.0 / D)
    w[0] = 1.0 / D
    inv = np.concatenate([w * np.cos(ang.T), -w * np.sin(ang.T)]).astype(np.float32)
    tok = np.zeros((P, TOPK, TILES), np.int32)
    tok[:, 0] = p[:, None] + P * np.arange(TILES)[None, :]
    tok[:, 1] = tok[:, 0] + TOKENS
    fill = np.zeros((2 * E * P, ROW), np.int32)
    fill[:, D] = 2 * TOKENS + np.arange(2 * E * P)
    sign = ((1.0 - 2.0 * (np.arange(D) % 2)) / D).astype(np.float32).reshape(1, D)
    return {"c_main": c, "c_sign": sign, "c_fwd": fwd, "c_inv": inv, "c_tok": tok.reshape(P, 2 * TILES), "c_fill": fill}


class Tally:

    def __init__(self, eng, sem):
        self.eng, self.sem, self.n, self.reg = eng, sem, 0, 0

    def link(self, ins):
        self.n += 1
        ins.then_inc(self.sem, 1)

    def settle(self):
        self.eng.wait_ge(self.sem, self.reg + self.n)


def run_steps(eng, step, lo, a, b, hi, unroll, tally=None, per_turn=0):
    for s in range(lo, a):
        step(s, s % unroll, s // unroll)
    n0 = tally.n if tally else 0
    with eng.Fori(0, (b - a) // unroll) as i:
        if tally:
            tally.reg = i * per_turn
        for u in range(unroll):
            step(i * unroll + (a + u), (a + u) % unroll, i + a // unroll)
    if tally:
        assert tally.n - n0 == per_turn, (tally.n - n0, per_turn)
        tally.reg = 0
        tally.n = n0 + per_turn * ((b - a) // unroll)
    for s in range(b, hi):
        step(s, s % unroll, s // unroll)


def inside(c, n):
    return not isinstance(c, int) or 0 <= c < n


def atleast(eng, sem, value):
    if not isinstance(value, int) or value > 0:
        eng.wait_ge(sem, value)


def build(nc, x, wq, wk, wv, rw, rb, sw1, sw3, sw2, ew1, ew2, c_main, c_fwd, c_inv, c_tok, c_fill, c_sign, out):
    ctx = ExitStack()
    with ctx:
        def sb(name, shape, dt):
            return ctx.enter_context(nc.sbuf_tensor(name, shape, dt))

        def sem(name):
            return ctx.enter_context(nc.semaphore(name))

        lists = nc.dram_tensor("lists", (E * CAP + E * P, ROW), F32, kind="Internal").ap()
        results = nc.dram_tensor("results", (2 * TOKENS + 2 * E * P, D), F32, kind="Internal").ap()

        X = sb("X", [P, TILES, D], F32)
        EW = {(w, h): sb(f"ew{w}_{h}", [P, E * KD * HR], F32R) for w in (1, 2) for h in "hl"}
        gates = sb("gates", [P, 2, TILES], F32)
        cst = sb("cst", [P, C_END], F32)
        tok = sb("tok", [P, 2 * TILES], I32)
        tri_b = sb("tri_b", [P, P], BF16)
        ones_b = sb("ones_b", [P, P], BF16)
        carry = sb("carry", [P, E], F32)
        table = sb("table", [1, 2 * BLOCKS + E], I32)
        st = sb("st", [P, 2, J, 6], F32)
        mv = sb("mv", [P, 2, J, 2], F32)
        rstd = sb("rstd", [P, 2, J], F32)
        half_neg = sb("half_neg", [P, J], F32)
        bias_r = sb("bias_r", [P, J, E], F32)
        ident = cst[:, C_ID:C_ID + P]
        tri_f = cst[:, C_TRI:C_TRI + P]
        ones_f = cst[:, C_ONE:C_ONE + P]

        region_at = (nc.sbuf_base + 31) // 32 * 32
        region_size = (nc.sbuf_usable_end - region_at) // 32 * 32 - 32
        sb("region", [P, region_size], mybir.dt.uint8)
        cursor = {}

        def place(phase, name, shape, dt, at=None):
            size = int(np.prod(shape[1:])) * (2 if dt == BF16 else 4)
            if at is None:
                at = cursor.get(phase, 0)
                cursor[phase] = (at + size + 31) // 32 * 32
            where[name] = at
            assert at + size <= region_size, (phase, name, at + size, region_size)
            return nc.alloc_sbuf_tensor_at(f"{phase}_{name}", shape, dt, offset=region_at + at)

        where = {}
        SW = {(w, h): place("a", f"sw{w}{h}", [P, 2 * FS], F32R) for w in (1, 3, 2) for h in "hl"}
        RW = {h: place("a", f"rw{h}", [P, KD, E], F32R) for h in "hl"}
        rows = place("a", "rows", [P, 2, J, ROW], F32)
        XT = {h: place("a", f"xt{h}", [P, 2, KD, N], F32R) for h in "hl"}
        U = {h: place("a", f"u{h}", [P, M, N], F32R) for h in "hl"}
        gate_u = place("a", "gate_u", [P, 2, N], F32)
        prob = place("a", "prob", [P, J, E], F32)
        small = place("a", "small", [P, 15, J, E], F32)
        slots = place("a", "slots", [P, 2, 2, J], I32)
        inc_b = place("a", "inc_b", [P, 2, E, J], BF16)
        raw_sw = {1: place("w", "raw_sw1", [P, 2 * FS], F32, where["rows"]),
                  3: place("w", "raw_sw3", [P, 2 * FS], F32, where["rows"] + 4 * 2 * FS),
                  2: place("w", "raw_sw2", [P, 2 * FS], F32, where["gate_u"])}
        raw_rw = place("w", "raw_rw", [E, D], F32, where["small"])
        raw_rb = place("w", "raw_rb", [1, J, E], F32, where["small"] + 4 * D)
        raw_ew = {1: place("w", "raw_ew1", [P, E, KD, HR], F32, where["xth"]),
                  2: place("w", "raw_ew2", [P, E, KD, HR], F32, where["uh"])}
        XB = place("b", "xb", [P, 4, 2, ROW], F32)
        XBT = {h: place("b", f"xbt{h}", [P, 2, KD, 2, P], F32R) for h in "hl"}
        HB = place("b", "hb", [P, 2, 2, HR], F32)
        HT = {h: place("b", f"ht{h}", [P, 2, KD, 2, P], F32R) for h in "hl"}
        YB = place("b", "yb", [P, 4, 2, D], F32)
        goal = place("b", "goal", [P, 4, 2], I32)
        over = place("b", "over", [1, E, TILES], F32)
        past = place("b", "past", [1, 2, BLOCKS, E], F32)
        line = place("b", "line", [1, 6, BLOCKS], F32)
        WF = {h: place("t", f"wf{h}", [P, KD, 3, NW], F32R) for h in "hl"}
        WI = {h: place("t", f"wi{h}", [P, 2, D], F32R) for h in "hl"}
        sign = place("t", "sign", [1, D], F32R)
        YG = place("t", "yg", [P, 2, J, D], F32)
        XN = place("t", "xn", [P, J, D], F32)
        XA = {h: place("t", f"xa{h}", [P, KD, N], F32R) for h in "hl"}
        FK = place("t", "fk", [P, 2, N], F32)
        PR = place("t", "pr", [P, 2, N], F32)
        FQ = place("t", "fq", [P, 2, N], F32)
        RN = place("t", "rn", [P, 2, N], F32)
        KV = place("t", "kv", [P, 2, N], F32)
        CUM = place("t", "cum", [P, 2, N], F32)
        ny = place("t", "ny", [P, 96], F32)
        PN = {h: place("t", f"pn{h}", [1, J, P], F32R) for h in "hl"}
        VH = {"h": place("t", "vhh", [P, 2, N], F32R, where["fk"]), "l": place("t", "vhl", [P, 2, N], F32R, where["pr"])}
        raw_w = [place("t", f"raw_w{i}", [P, KD, D], F32, where["yg"] + i * 4 * KD * D) for i in range(3)]
        raw_fwd = place("t", "raw_fwd", [P, KD, NW], F32, where["xn"])
        raw_inv = place("t", "raw_inv", [P, 2, D], F32, where["yg"] + 3 * 4 * KD * D)
        raw_sign = place("t", "raw_sign", [1, D], F32, where["xn"] + 4 * KD * NW + 16)
        YF = place("f", "yf", [P, 2, 2, J, D], F32)

        bank = ctx.enter_context(nc.psum_tensor("bank", [P, 8, 512], F32))

        def apart(eng):
            eng.sem_inc(s_passed, 1)

        s_passed = sem("passed")

        s_const, s_small, s_raw, s_raw_e = sem("const_in"), sem("small_ok"), sem("raw_in"), [sem("raw_e1"), sem("raw_e2")]
        s_whi, s_wlo, s_ehi, s_elo, s_rps = sem("w_hi"), sem("w_lo"), sem("e_hi"), sem("e_lo"), sem("router_w_ps")
        s_spare, s_mat, s_mps, s_mhi, s_mlo = sem("spare_rows"), sem("mat_in"), sem("mat_ps"), sem("mat_hi"), sem("mat_lo")
        s_x = [sem("x_in0"), sem("x_in1")]
        s_var, s_rstd = sem("var_ok"), sem("rstd_ok")
        s_xn, s_tps, s_xh, s_xl = sem("xn_ok"), sem("xt_ps"), sem("xt_h"), sem("xt_l")
        s_logit, s_prob, s_mask, s_rank, s_slot = (sem("logits"), sem("prob_ok"), sem("mask_ok"), sem("rank_ps"),
                                                   sem("slots_ok"))
        s_hps, s_sig, s_u, s_uh, s_ul = sem("h_ps"), sem("sig_ok"), sem("u_ok"), sem("u_hi"), sem("u_lo")
        s_ops, s_xout, s_scat = sem("o_ps"), sem("x_out"), sem("scattered")
        s_table, s_tail = sem("table_ok"), sem("tail_rows")
        s_xb = [sem(f"xb_in{i}") for i in range(4)]
        s_bps, s_bh, s_bl, s_mm1, s_gelu = sem("xb_ps"), sem("xb_h"), sem("xb_l"), sem("h1_ps"), sem("gelu_ok")
        s_hT, s_hh, s_hl, s_yps, s_yok = sem("ht_ps"), sem("ht_h"), sem("ht_l"), sem("y_ps"), sem("y_ok")
        s_ysc = [sem(f"y_out{i}") for i in range(4)]
        s_yg, s_comb, s_txn, s_add, s_atp, s_ah, s_al = (sem("yg_in"), sem("combined"), sem("a_xn"), sem("a_added"),
                                                         sem("a_xt_ps"), sem("a_xt_h"), sem("a_xt_l"))
        s_kps, s_vps, s_nps, s_qps = sem("k_ps"), sem("v_ps"), sem("nyq_ps"), sem("q_ps")
        s_kev, s_ksum, s_kroot, s_vused, s_kvd = sem("k_out"), sem("k_sum"), sem("k_root"), sem("v_used"), sem("kv_done")
        s_qc, s_qev, s_qsum, s_qroot, s_p, s_ph, s_pl = (sem("q_copy"), sem("q_out"), sem("q_sum"), sem("q_root"),
                                                         sem("p_ok"), sem("p_h"), sem("p_l"))
        s_nkv, s_nsum, s_npq, s_nt, s_nh, s_nl = (sem("nyq_kv"), sem("nyq_sum"), sem("nyq_pq"), sem("nyq_t"),
                                                  sem("nyq_h"), sem("nyq_l"))
        s_aps, s_aout = sem("a_ps"), sem("a_out")
        s_f = [sem("f_in0"), sem("f_in1")]
        s_fc, s_store = sem("f_combined"), sem("stored")
        s_dve, s_pool = sem("dve_chain"), sem("pool_chain")

        x_d = x.rearrange("b s d -> (b s) d").rearrange("(t p) d -> p t d", p=P)
        out_d = out.rearrange("b s d -> (b s) d").rearrange("(t p) d -> p t d", p=P)
        res_d = results[0:2 * TOKENS, :].rearrange("(k t p) d -> p k t d", p=P, k=2)
        YW = PAIRS // 4 * 32

        block = ctx.enter_context(nc.Block())

        @block.sync
        def _(sp):
            sp.dma_start(cst[:], c_main).then_inc(s_const, 16)
            sp.dma_start(tok[:], c_tok).then_inc(s_const, 16)

            def shared_weights():
                sp.dma_start(raw_rw[:], rw).then_inc(s_raw, 16)
                for j in range(J):
                    sp.dma_start(raw_rb[:, j, :], rb.rearrange("(a e) -> a e", a=1)).then_inc(s_raw, 16)
                for w, src in ((1, sw1), (3, sw3), (2, sw2)):
                    k = KD if w != 2 else M
                    sp.dma_start(raw_sw[w][:].rearrange("p (k n) -> p k n", k=k),
                                 src.rearrange("(k p) n -> p k n", p=P)).then_inc(s_raw, 16)

            shared_weights()
            for i, src in enumerate((ew1, ew2)):
                sp.dma_start(raw_ew[i + 1][:].rearrange("p e k n -> p (e k) n"),
                             src.rearrange("e (k p) n -> p (e k) n", p=P)).then_inc(s_raw_e[i], 16)
            fill = c_fill.bitcast(F32)
            sp.dma_start(lists[E * CAP:E * CAP + E * P, :], fill[E * P:2 * E * P, :]).then_inc(s_spare, 16)

            def load_x(c, par, half):
                atleast(sp, s_x[par], half * 16)
                sp.dma_start(X[:, bass.ds(c * J, J), :], x_d[:, bass.ds(c * J, J), :]).then_inc(s_x[par], 16)

            run_steps(sp, load_x, 0, 2, CH, CH, 2)

            def phase_b(layer):
                sp.wait_ge(s_table, layer + 1)
                for e in range(E):
                    end = sp.value_load(table[0:1, 2 * BLOCKS + e:2 * BLOCKS + e + 1], min_val=e * CAP,
                                        max_val=e * CAP + TOKENS)
                    sp.dma_start(lists[bass.ds(end, P), :], fill[e * P:(e + 1) * P, :]).then_inc(s_tail, 16)
                sp.wait_ge(s_tail, E * 16 * (layer + 1))
                sp.wait_ge(s_spare, 16)
                sp.wait_ge(s_scat, 2 * J * 16 * CH * (layer + 1))
                p0 = PAIRS * layer

                def step(n, slot, q):
                    atleast(sp, s_bl, n + (p0 - 3) if not isinstance(n, int) or n >= 4 else 0)
                    for blk in range(2):
                        row = sp.value_load(table[0:1, bass.ds(n * 2 + blk, 1)], min_val=0,
                                            max_val=E * CAP + (E - 1) * P)
                        sp.dma_start(XB[:, slot, blk, :], lists[bass.ds(row, P), :]).then_inc(s_xb[slot], 16)

                run_steps(sp, step, 0, 4, PAIRS, PAIRS, 4)

            def results_in(layer):
                for i in range(4):
                    sp.wait_ge(s_ysc[i], YW * (layer + 1))

            phase_b(0)
            results_in(0)
            for i, src in enumerate((wk, wv, wq)):
                sp.dma_start(raw_w[i][:], src.rearrange("(k p) n -> p k n", p=P)).then_inc(s_mat, 16)
            sp.dma_start(raw_fwd[:], c_fwd.rearrange("(k p) n -> p k n", p=P)).then_inc(s_mat, 16)
            sp.dma_start(raw_inv[:], c_inv.rearrange("(k p) n -> p k n", p=P)).then_inc(s_mat, 16)
            sp.dma_start(raw_sign[:], c_sign).then_inc(s_mat, 16)
            sp.wait_ge(s_mlo, 3)

            def load_results(c, par, half):
                atleast(sp, s_comb, c)
                for k in range(2):
                    sp.dma_start(YG[:, k, :, :], res_d[:, k, bass.ds(c * J, J), :]).then_inc(s_yg, 16)

            run_steps(sp, load_results, 0, 2, CH, CH, 2)
            sp.wait_ge(s_aout, 2 * CH)
            shared_weights()
            phase_b(1)
            results_in(1)
            def load_last(c, par, half):
                atleast(sp, s_fc, c - 1)
                for k in range(2):
                    sp.dma_start(YF[:, par, k, :, :], res_d[:, k, bass.ds(c * J, J), :]).then_inc(s_f[par], 16)

            sp.wait_ge(s_yok, 2 * PAIRS)
            run_steps(sp, load_last, 0, 2, CH, CH, 2)
            sp.wait_ge(s_store, 16 * CH)

        @block.gpsimd
        def _(pool):
            ch = Tally(pool, s_pool)

            def rstd_of(par, count):
                pool.wait_ge(s_var, count)
                apart(pool)
                ch.link(pool.tensor_scalar(rstd[:, par, :], mv[:, par, :, 1], LN_EPS, 1.0, ALU.add, ALU.mult))
                ch.settle()
                pool.tensor_tensor(rstd[:, par, :], rstd[:, par, :], half_neg[:, :], ALU.pow).then_inc(s_rstd, 1)

            def phase_a(layer):
                g0, v0 = CH * layer, 2 * CH * layer

                def step(s, par, half):
                    if inside(s + 2, CH):
                        rstd_of(par, s + (v0 + 3))
                    if inside(s + 1, CH):
                        c, g, q = s + 1, s + (g0 + 1), 1 - par
                        pool.wait_ge(s_slot, g + 1)
                        for k in range(TOPK):
                            atleast(pool, s_scat, g * 128 + 64 * k)
                            ch.link(pool.tensor_copy(rows[:, q, :, D:D + 1].bitcast(I32),
                                                     tok[:, bass.ds(c * J + k * TILES, J)].unsqueeze(2)))
                            ch.settle()
                            apart(pool)
                            for j in range(J):
                                pool.indirect_dma_start(
                                    out=lists, out_offset=bass.IndirectOffsetOnAxis(ap=slots[:, q, k, j:j + 1], axis=0),
                                    in_=rows[:, q, j, :], in_offset=None).then_inc(s_scat, 16)

                run_steps(pool, step, -2, 2, CH - 2, CH, 2, ch, 6)

            def phase_b(layer):
                def step(n, slot, q):
                    pool.wait_ge(s_yok, n + (PAIRS * layer + 1))
                    apart(pool)
                    for blk in range(2):
                        pool.indirect_dma_start(
                            out=results,
                            out_offset=bass.IndirectOffsetOnAxis(ap=goal[:, slot, blk:blk + 1], axis=0),
                            in_=YB[:, slot, blk, :], in_offset=None).then_inc(s_ysc[slot], 16)

                run_steps(pool, step, 0, 4, PAIRS, PAIRS, 4)

            pool.wait_ge(s_small, 1)
            phase_a(0)
            phase_b(0)

            def attention(s, par, half):
                if inside(s + 1, CH):
                    c, q = s + 1, 1 - par
                    rstd_of(q, s + (CH + 2))
                    pool.wait_ge(s_txn, c + 1)
                    xc = X[:, bass.ds(c * J, J), :]
                    pool.tensor_tensor(xc, xc, XN[:], ALU.add).then_inc(s_add, 1)

            run_steps(pool, attention, -1, 2, CH - 2, CH, 2, ch, 2)
            phase_a(1)
            phase_b(1)

        @block.scalar
        def _(act):
            def copy(o, i):
                return act.activation(o, i, ACT.Copy)

            def shared_weights(layer):
                act.wait_ge(s_raw, 128 * (layer + 1))
                for w in (1, 3, 2):
                    copy(SW[w, "h"][:], raw_sw[w][:]).then_inc(s_whi, 1)
                act.wait_ge(s_rps, 2 * layer + 1)
                copy(RW["h"][:], bank[:, 7, 0:KD * E].rearrange("p (k e) -> p k e", k=KD)).then_inc(s_whi, 1)

            def phase_a(layer):
                g0 = CH * layer

                def sigmoid_gate(s, m):
                    n = s * M + (g0 * M + m)
                    act.wait_ge(s_hps, n + 1)
                    atleast(act, s_ul, n - 1)
                    act.activation(gate_u[:, m % 2, :], bank[:, 2 + 2 * (m % 2), :], ACT.Sigmoid).then_inc(s_sig, 1)

                def high_u(s, m):
                    n = s * M + (g0 * M + m)
                    act.wait_ge(s_u, n + 1)
                    if m == 0:
                        atleast(act, s_ops, s * 2 + 2 * g0)
                    copy(U["h"][:, m, :], gate_u[:, m % 2, :]).then_inc(s_uh, 1)

                def step(s, par, half):
                    now, nxt = inside(s, CH), inside(s + 1, CH)
                    if now:
                        sigmoid_gate(s, 0)
                        sigmoid_gate(s, 1)
                        high_u(s, 0)
                    if nxt:
                        g = s + (g0 + 1)
                        act.wait_ge(s_tps, g + 1)
                        copy(XT["h"][:, 1 - par, :, :], bank[:, 0:2, :]).then_inc(s_xh, 1)
                    if now:
                        sigmoid_gate(s, 2)
                        high_u(s, 1)
                    if nxt:
                        act.wait_ge(s_logit, g + 1)
                        act.activation(prob[:].rearrange("p j e -> p (j e)"), bank[:, 7, 0:J * E],
                                       ACT.Sigmoid).then_inc(s_prob, 1)
                    if now:
                        sigmoid_gate(s, 3)
                        high_u(s, 2)
                        high_u(s, 3)

                run_steps(act, step, -1, 2, CH - 2, CH, 2)

            def expert_weights():
                for w in (1, 2):
                    act.wait_ge(s_raw_e[w - 1], 16)
                    raw = raw_ew[w][:].rearrange("p e k n -> p (e k n)")
                    for i in range(0, E * KD * HR, 1024):
                        copy(EW[w, "h"][:, i:i + 1024], raw[:, i:i + 1024]).then_inc(s_ehi, 1)

            def phase_b(layer):
                p0 = PAIRS * layer

                def step(s, u, q):
                    par = u % 2
                    if inside(s - 1, PAIRS):
                        act.wait_ge(s_hT, s + p0)
                        copy(HT["h"][:, 1 - par].rearrange("p k b t -> p (k b t)"),
                             bank[:, 4 + 1 - par, :]).then_inc(s_hh, 1)
                    if inside(s + 1, PAIRS):
                        act.wait_ge(s_bps, s + (p0 + 2))
                        copy(XBT["h"][:, 1 - par].rearrange("p k b t -> p (k b t)"),
                             bank[:, 1 - par, :]).then_inc(s_bh, 1)
                    if inside(s, PAIRS):
                        act.wait_ge(s_mm1, s + (p0 + 1))
                        act.activation(HB[:, par].rearrange("p b n -> p (b n)"), bank[:, 2 + par, :],
                                       ACT.Gelu).then_inc(s_gelu, 1)

                run_steps(act, step, -1, 4, PAIRS - 4, PAIRS + 1, 4)

            def attention(s, par, half):
                if inside(s, CH):
                    act.wait_ge(s_kps, s + 1)
                    copy(FK[:], bank[:, 2:4, :]).then_inc(s_kev, 1)
                    act.activation(PR[:], bank[:, 2:4, :], ACT.Square).then_inc(s_kev, 1)
                    act.wait_ge(s_ksum, s + 1)
                    act.activation(RN[:, 0, :], RN[:, 0, :], ACT.Sqrt).then_inc(s_kroot, 1)
                    act.wait_ge(s_qps, s + 1)
                    copy(FQ[:], bank[:, 2:4, :]).then_inc(s_qc, 1)
                    act.wait_ge(s_kvd, s + 1)
                    act.activation(PR[:], bank[:, 2:4, :], ACT.Square).then_inc(s_qev, 1)
                    act.wait_ge(s_qsum, s + 1)
                    act.activation(RN[:, 1, :], RN[:, 1, :], ACT.Sqrt).then_inc(s_qroot, 1)
                if inside(s + 1, CH):
                    act.wait_ge(s_atp, s + 2)
                    copy(XA["h"][:], bank[:, 0:2, :]).then_inc(s_ah, 1)
                if inside(s, CH):
                    act.wait_ge(s_nt, s + 1)
                    copy(PN["h"][:].rearrange("p j t -> p (j t)"), bank[0:1, 5, :]).then_inc(s_nh, 1)
                    act.wait_ge(s_p, s + 1)
                    copy(VH["h"][:], KV[:]).then_inc(s_ph, 1)

            shared_weights(0)
            expert_weights()
            phase_a(0)
            phase_b(0)
            act.wait_ge(s_mat, 96)
            copy(WI["h"][:], raw_inv[:]).then_inc(s_mhi, 1)
            copy(sign[:], raw_sign[:]).then_inc(s_mhi, 1)
            for i in range(3):
                for k in range(KD):
                    act.wait_ge(s_mps, 2 * i + k + 1)
                    copy(WF["h"][:, k, i, :], bank[:, 2 * i + k, 0:NW]).then_inc(s_mhi, 1)
            run_steps(act, attention, -1, 2, CH - 2, CH, 2)
            shared_weights(1)
            phase_a(1)
            phase_b(1)

            def store(c, par, half):
                act.wait_ge(s_fc, c + 1)
                act.dma_start(out_d[:, bass.ds(c * J, J), :], X[:, bass.ds(c * J, J), :]).then_inc(s_store, 16)

            run_steps(act, store, 0, 2, CH, CH, 2)

        @block.tensor
        def _(pe):
            def three(o, a, b, first, last):
                pe.matmul(o, a("h"), b("h"), start=first, stop=False)
                pe.matmul(o, a("h"), b("l"), start=False, stop=False)
                return pe.matmul(o, a("l"), b("h"), start=False, stop=last)

            def shared_weights(layer):
                pe.wait_ge(s_raw, 128 * (layer + 1))
                pe.wait_ge(s_const, 32)
                for k in range(KD):
                    ins = pe.transpose(bank[:, 7, k * E:(k + 1) * E], raw_rw[:, k * P:(k + 1) * P], ident[0:E, 0:E])
                ins.then_inc(s_rps, 1)
                if layer == 0:
                    pe.matmul(bank[:, 6, 0:J * E], ones_f[0:1, :], raw_rb[:].rearrange("p j e -> p (j e)"),
                              start=True, stop=True).then_inc(s_rps, 1)

            def phase_a(layer):
                g0 = CH * layer

                def transposes(c, par):
                    g = c + g0
                    pe.wait_ge(s_xn, g + 1)
                    atleast(pe, s_xl, g)
                    atleast(pe, s_xout, (g - 1) * 2)
                    for k in range(KD):
                        for j in range(J):
                            ins = pe.transpose(bank[:, k, j * P:(j + 1) * P], rows[:, par, j, k * P:(k + 1) * P], ident)
                    ins.then_inc(s_tps, 1)

                def router(c, par):
                    g = c + g0
                    pe.wait_ge(s_xl, g + 1)
                    for j in range(J):
                        for k in range(KD):
                            ins = three(bank[:, 7, j * E:(j + 1) * E], lambda h: XT[h][:, par, k, j * P:(j + 1) * P],
                                        lambda h: RW[h][:, k, :], k == 0, k == KD - 1)
                    ins.then_inc(s_logit, 1)

                def ranks(c, par):
                    g = c + g0
                    pe.wait_ge(s_mask, g + 1)
                    atleast(pe, s_slot, g)
                    pe.matmul(bank[:, 7, 64:64 + J * E], tri_b[:], inc_b[:, 0].rearrange("p e j -> p (e j)"),
                              start=True, stop=False)
                    pe.matmul(bank[:, 7, 64:64 + J * E], ones_b[:], inc_b[:, 1].rearrange("p e j -> p (e j)"),
                              start=False, stop=True)
                    pe.matmul(bank[:, 7, 128:128 + E], ones_b[:], inc_b[:, 1, :, J - 1], start=True,
                              stop=True).then_inc(s_rank, 1)

                def hidden(c, par, m):
                    n = c * M + (g0 * M + m)
                    atleast(pe, s_u, n - 1)
                    for w, o in ((1, 2 + 2 * (m % 2)), (3, 3 + 2 * (m % 2))):
                        for k in range(KD):
                            ins = three(bank[:, o, :], lambda h: SW[w, h][:, k * FS + m * P:k * FS + (m + 1) * P],
                                        lambda h: XT[h][:, par, k, :], k == 0, k == KD - 1)
                    ins.then_inc(s_hps, 1)

                def down(c, par, half):
                    g = c + g0
                    if half == 0:
                        pe.wait_ge(s_ul, g * M + M)
                        atleast(pe, s_xout, g * 2 - 1)
                    for i in range(2):
                        j = 2 * half + i
                        for m in range(M):
                            ins = three(bank[:, 6 if half == 0 else 0, i * D:(i + 1) * D],
                                        lambda h: U[h][:, m, j * P:(j + 1) * P],
                                        lambda h: SW[2, h][:, m * D:(m + 1) * D], m == 0, m == M - 1)
                    ins.then_inc(s_ops, 1)

                def step(s, par, half):
                    now, nxt = inside(s, CH), inside(s + 1, CH)
                    if now:
                        hidden(s, par, 0)
                        hidden(s, par, 1)
                    if nxt:
                        transposes(s + 1, 1 - par)
                    if now:
                        hidden(s, par, 2)
                    if nxt:
                        router(s + 1, 1 - par)
                    if now:
                        hidden(s, par, 3)
                    if nxt:
                        ranks(s + 1, 1 - par)
                    if now:
                        down(s, par, 0)
                        down(s, par, 1)

                pe.wait_ge(s_wlo, 4 * (layer + 1))
                run_steps(pe, step, -1, 2, CH - 2, CH, 2)

            def phase_b(layer):
                p0 = PAIRS * layer

                def load_experts(s, par):
                    for blk in range(2):
                        pe.reg_load(offset[par][blk], table[0:1, bass.ds(s * 2 + (BLOCKS + blk), 1)])

                def weights_at(par):
                    return [pe.snap(offset[par][blk], min_val=0, max_val=E - 1) for blk in range(2)]

                def expert(w, h, e, k):
                    v = EW[w, h][:].rearrange("p (e n) -> p e n", e=E)
                    return v[:, bass.ds(e, 1), k * HR:(k + 1) * HR].rearrange("p a n -> p (a n)")

                def step(s, u, q):
                    par = u % 2
                    if inside(s - 1, PAIRS):
                        pe.wait_ge(s_gelu, s + p0)
                        atleast(pe, s_hl, s + (p0 - 2))
                        for k in range(KD):
                            for blk in range(2):
                                ins = pe.transpose(bank[:, 5 - par, (2 * k + blk) * P:(2 * k + blk + 1) * P],
                                                   HB[:, 1 - par, blk, k * P:(k + 1) * P], ident)
                        ins.then_inc(s_hT, 1)
                    if inside(s + 1, PAIRS):
                        slot = (u + 1) % 4
                        turn = q if u < 3 else q + 1
                        pe.wait_ge(s_xb[slot], turn * 32 + (YW * layer + 32))
                        atleast(pe, s_bl, s + p0)
                        for k in range(KD):
                            for blk in range(2):
                                ins = pe.transpose(bank[:, 1 - par, (2 * k + blk) * P:(2 * k + blk + 1) * P],
                                                   XB[:, slot, blk, k * P:(k + 1) * P], ident)
                        ins.then_inc(s_bps, 1)
                    if inside(s, PAIRS):
                        at = weights_at(par)
                        pe.wait_ge(s_bl, s + (p0 + 1))
                        atleast(pe, s_gelu, s + (p0 - 1))
                        for blk in range(2):
                            for k in range(KD):
                                ins = three(bank[:, 2 + par, blk * HR:(blk + 1) * HR],
                                            lambda h: XBT[h][:, par, k, blk, :],
                                            lambda h: expert(1, h, at[blk], k), k == 0, k == KD - 1)
                        ins.then_inc(s_mm1, 1)
                    if inside(s - 1, PAIRS):
                        at = weights_at(1 - par)
                        pe.wait_ge(s_hl, s + p0)
                        atleast(pe, s_yok, s + (p0 - 2))
                        for blk in range(2):
                            for k in range(KD):
                                ins = three(bank[:, 7 - par, blk * D:(blk + 1) * D],
                                            lambda h: HT[h][:, 1 - par, k, blk, :],
                                            lambda h: expert(2, h, at[blk], k), k == 0, k == KD - 1)
                        ins.then_inc(s_yps, 1)
                    if inside(s + 1, PAIRS):
                        load_experts(s + 1, 1 - par)

                pe.wait_ge(s_table, layer + 1)
                offset = [[pe.alloc_register(f"expert_{layer}_{par}_{blk}") for blk in range(2)] for par in range(2)]
                run_steps(pe, step, -1, 4, PAIRS - 4, PAIRS + 1, 4)

            def attention_weights():
                pe.wait_ge(s_mat, 96)
                for i in range(3):
                    for m in range(KD):
                        for k in range(KD):
                            ins = pe.matmul(bank[:, 2 * i + m, 0:NW], raw_w[i][:, k, m * P:(m + 1) * P],
                                            raw_fwd[:, k, :], start=(k == 0), stop=(k == KD - 1))
                        ins.then_inc(s_mps, 1)

            def attention(s, par, half):
                def spectrum(i, to, done):
                    for r in range(2):
                        for k in range(KD):
                            ins = three(bank[:, to + r, :], lambda h: WF[h][:, k, i, r * NF:(r + 1) * NF],
                                        lambda h: XA[h][:, k, :], k == 0, k == KD - 1)
                    ins.then_inc(done, 1)

                now = inside(s, CH)
                if now:
                    pe.wait_ge(s_al, s + 1)
                    spectrum(0, 2, s_kps)
                    atleast(pe, s_aout, s * 2)
                    spectrum(1, 4, s_vps)
                    for j in range(J):
                        for k in range(KD):
                            ins = three(bank[:, 7, j * 6:(j + 1) * 6].rearrange("p (a b) -> p a b", a=3),
                                        lambda h: XA[h][:, k, j * P:(j + 1) * P],
                                        lambda h: WF[h][:, k, :, D:NW], k == 0, k == KD - 1)
                    ins.then_inc(s_nps, 1)
                    pe.wait_ge(s_kev, s * 2 + 2)
                    spectrum(2, 2, s_qps)
                    pe.wait_ge(s_nkv, s + 1)
                    pe.matmul(bank[:, 7, 32:32 + J], tri_f, ny[:, 64:64 + J], start=True, stop=False)
                    pe.matmul(bank[:, 7, 32:32 + J], ones_f, ny[:, 72:72 + J], start=False, stop=True).then_inc(s_nsum, 1)
                if inside(s + 1, CH):
                    pe.wait_ge(s_txn, s + 2)
                    if isinstance(s, int) and s < 0:
                        pe.wait_ge(s_mlo, 3)
                    atleast(pe, s_al, s + 1)
                    for k in range(KD):
                        for j in range(J):
                            ins = pe.transpose(bank[:, k, j * P:(j + 1) * P], XN[:, j, k * P:(k + 1) * P], ident)
                    ins.then_inc(s_atp, 1)
                if now:
                    pe.wait_ge(s_npq, s + 1)
                    pe.wait_ge(s_vused, s + 1)
                    for j in range(J):
                        ins = pe.transpose(bank[0:1, 5, j * P:(j + 1) * P], ny[:, 80 + j:81 + j], ident)
                    ins.then_inc(s_nt, 1)
                    pe.wait_ge(s_pl, s + 1)
                    pe.wait_ge(s_nl, s + 1)
                    for half_ in range(2):
                        for i in range(2):
                            j = 2 * half_ + i
                            o = bank[:, 6 if half_ == 0 else 4, i * D:(i + 1) * D]
                            for r in range(2):
                                three(o, lambda h: VH[h][:, r, j * P:(j + 1) * P], lambda h: WI[h][:, r, :],
                                      r == 0, False)
                            pe.matmul(o, PN["h"][:, j, :], sign[:], start=False, stop=False)
                            ins = pe.matmul(o, PN["l"][:, j, :], sign[:], start=False, stop=True)
                        ins.then_inc(s_aps, 1)

            shared_weights(0)
            phase_a(0)
            pe.wait_ge(s_elo, 8)
            phase_b(0)
            attention_weights()
            run_steps(pe, attention, -1, 2, CH - 2, CH, 2)
            shared_weights(1)
            phase_a(1)
            phase_b(1)

        @block.vector
        def _(dve):
            ch = Tally(dve, s_dve)

            def low(o, v, h):
                return dve.tensor_tensor(o, v, h.bitcast(F32), ALU.subtract)

            def bc(a, n):
                return a.to_broadcast(n)

            def stats(c, par):
                for j in range(J):
                    ch.link(dve.bn_stats(st[:, par, j, :], X[:, bass.ds(c * J + j, 1), :].rearrange("p a d -> p (a d)")))
                ch.settle()
                apart(dve)
                for j in range(J):
                    ins = dve.bn_aggr(mv[:, par, j, :], st[:, par, j, :])
                ins.then_inc(s_var, 1)

            def normalise(c, par, to, count, done):
                dve.wait_ge(s_rstd, count)
                for j in range(J):
                    ins = dve.tensor_scalar(to[:, j, 0:D], X[:, bass.ds(c * J + j, 1), :].rearrange("p a d -> p (a d)"),
                                            mv[:, par, j, 0:1], rstd[:, par, j:j + 1], ALU.subtract, ALU.mult)
                ins.then_inc(done, 1)

            def shared_weights(layer):
                for i, w in enumerate((1, 3, 2)):
                    dve.wait_ge(s_whi, 4 * layer + i + 1)
                    low(SW[w, "l"][:], raw_sw[w][:], SW[w, "h"][:]).then_inc(s_wlo, 1)
                dve.wait_ge(s_whi, 4 * layer + 4)
                low(RW["l"][:], bank[:, 7, 0:KD * E].rearrange("p (k e) -> p k e", k=KD), RW["h"][:]).then_inc(s_wlo, 1)
                if layer == 0:
                    dve.wait_ge(s_rps, 2)
                    ch.link(dve.tensor_copy(bias_r[:].rearrange("p j e -> p (j e)"), bank[:, 6, 0:J * E]))

            def phase_a(layer):
                g0, v0 = CH * layer, 2 * CH * layer
                flat = "p j e -> p (j e)"
                (sel, gt, eq, rk, msk, cnt, pick2, slotv, prod2) = (small[:, 0], small[:, 1], small[:, 2], small[:, 3],
                                                                    small[:, 4], small[:, 5], small[:, 6:8],
                                                                    small[:, 8], small[:, 9:11])
                m8, few = small[:, 11], small[:, 12].rearrange(flat)
                gsum = small[:, 13].rearrange(flat)
                res_e, res_j = cst[:, C_RESE:C_RESE + J * E], cst[:, C_RESJ:C_RESJ + J * E]

                def route(c, par):
                    g = c + g0
                    dve.wait_ge(s_prob, g + 1)
                    ch.link(dve.tensor_tensor(sel, prob[:], bias_r[:], ALU.add))
                    ch.settle()
                    apart(dve)
                    for j in range(J):
                        ch.link(dve.max(m8[:, j, :], sel[:, j, :]))
                    ch.settle()
                    second = bc(m8[:, :, 1:2], [P, J, E])
                    ch.link(dve.tensor_tensor(gt, sel, second, ALU.is_gt))
                    ch.link(dve.tensor_tensor(eq, sel, second, ALU.is_equal))
                    ch.settle()
                    ch.link(dve.tensor_reduce(few[:, 0:J], gt, AX.X, ALU.add))
                    ch.link(dve.tensor_tensor_scan(rk.rearrange(flat), res_e, eq.rearrange(flat), 0.0, ALU.mult, ALU.add))
                    ch.settle()
                    ch.link(dve.tensor_tensor(rk, rk, bc(few[:, 0:J].unsqueeze(2), [P, J, E]), ALU.add))
                    ch.settle()
                    ch.link(dve.scalar_tensor_tensor(eq, rk, float(TOPK), eq, ALU.is_le, ALU.mult))
                    ch.settle()
                    ch.link(dve.tensor_tensor(msk, gt, eq, ALU.add))
                    ch.settle()
                    ch.link(dve.tensor_copy(inc_b[:, 0].rearrange("p e j -> p j e"), msk))
                    ch.link(dve.tensor_copy(slotv.rearrange(flat).rearrange("p (e j) -> p j e", e=E), msk))
                    ch.link(dve.tensor_tensor_scan(cnt.rearrange(flat), res_e, msk.rearrange(flat), 0.0,
                                                   ALU.mult, ALU.add))
                    ch.settle()
                    dve.tensor_tensor_scan(inc_b[:, 1].rearrange("p e j -> p (e j)"), res_j,
                                           slotv.rearrange(flat), 0.0, ALU.mult, ALU.add).then_inc(s_mask, 1)
                    ch.link(dve.scalar_tensor_tensor(pick2[:, 0], cnt, 1.0, msk, ALU.is_equal, ALU.mult))
                    ch.settle()
                    ch.link(dve.tensor_tensor(pick2[:, 1], msk, pick2[:, 0], ALU.subtract))
                    ch.settle()
                    for k in range(TOPK):
                        ch.link(dve.tensor_tensor(prod2[:, k], pick2[:, k], prob[:], ALU.mult))
                    ch.settle()
                    ch.link(dve.tensor_reduce(gsum[:, 0:2 * J].rearrange("p (k j) -> p k j", k=2), prod2, AX.X, ALU.add))
                    ch.settle()
                    ch.link(dve.tensor_tensor(gsum[:, 8:12], gsum[:, 0:J], gsum[:, J:2 * J], ALU.add))
                    ch.settle()
                    ch.link(dve.tensor_scalar(gsum[:, 12:16], gsum[:, 8:12], GATE_EPS, 0.5, ALU.is_gt, ALU.mult))
                    ch.link(dve.tensor_scalar(gsum[:, 16:20], gsum[:, 8:12], GATE_EPS, None, ALU.add))
                    ch.settle()
                    ch.link(dve.reciprocal(gsum[:, 16:20], gsum[:, 16:20]))
                    ch.link(dve.tensor_scalar(gsum[:, 20:24], gsum[:, 12:16], -1.0 / TOPK, 0.5 / TOPK,
                                              ALU.mult, ALU.add))
                    ch.settle()
                    ch.link(dve.tensor_tensor(gsum[:, 16:20], gsum[:, 16:20], gsum[:, 12:16], ALU.mult))
                    ch.settle()
                    for k in range(TOPK):
                        ch.link(dve.tensor_tensor(gsum[:, 4 * k:4 * k + 4], gsum[:, 4 * k:4 * k + 4], gsum[:, 16:20],
                                                  ALU.mult))
                    ch.settle()
                    for k in range(TOPK):
                        ch.link(dve.tensor_tensor(gates[:, k, bass.ds(c * J, J)], gsum[:, 4 * k:4 * k + 4],
                                                  gsum[:, 20:24], ALU.add))

                def places(c, par):
                    g = c + g0
                    dve.wait_ge(s_rank, g + 1)
                    ch.link(dve.tensor_tensor(slotv,
                                              bank[:, 7, 64:64 + J * E].rearrange("p (e j) -> p j e", e=E),
                                              bc(carry[:].unsqueeze(1), [P, J, E]), ALU.add))
                    ch.settle()
                    ch.link(dve.tensor_tensor(carry[:], carry[:], bank[:, 7, 128:128 + E], ALU.add))
                    for k in range(TOPK):
                        ch.link(dve.tensor_tensor(prod2[:, k], pick2[:, k], slotv, ALU.mult))
                    ch.settle()
                    ch.link(dve.tensor_reduce(few[:, 8:8 + 2 * J].rearrange("p (k j) -> p k j", k=2), prod2, AX.X, ALU.add))
                    ch.settle()
                    dve.tensor_copy(slots[:, par], few[:, 8:8 + 2 * J].rearrange("p (k j) -> p k j",
                                                                                 k=2)).then_inc(s_slot, 1)

                def hidden(s, m):
                    n = s * M + (g0 * M + m)
                    gu = gate_u[:, m % 2, :]
                    dve.wait_ge(s_sig, n + 1)
                    ch.link(dve.tensor_tensor(gu, gu, bank[:, 2 + 2 * (m % 2), :], ALU.mult))
                    ch.settle()
                    dve.tensor_tensor(gu, gu, bank[:, 3 + 2 * (m % 2), :], ALU.mult).then_inc(s_u, 1)

                def low_u(s, m):
                    n = s * M + (g0 * M + m)
                    dve.wait_ge(s_uh, n + 1)
                    low(U["l"][:, m, :], gate_u[:, m % 2, :], U["h"][:, m, :]).then_inc(s_ul, 1)

                def step(s, par, half):
                    now, nxt, far = inside(s, CH), inside(s + 1, CH), inside(s + 2, CH)
                    if now:
                        hidden(s, 0)
                        hidden(s, 1)
                        low_u(s, 0)
                    if nxt:
                        dve.wait_ge(s_xh, s + (g0 + 2))
                        low(XT["l"][:, 1 - par], bank[:, 0:2, :], XT["h"][:, 1 - par]).then_inc(s_xl, 1)
                    if far:
                        if layer == 0:
                            dve.wait_ge(s_x[par], half * 16 + 32)
                            apart(dve)
                        stats(s + 2, par)
                    if now:
                        hidden(s, 2)
                        low_u(s, 1)
                    if nxt:
                        route(s + 1, 1 - par)
                    if now:
                        hidden(s, 3)
                        low_u(s, 2)
                    if far:
                        atleast(dve, s_scat, (s + (g0 + 1)) * 128 if inside(s, CH) else 128 * g0)
                        normalise(s + 2, par, rows[:, par], s + (v0 + 3), s_xn)
                    if now:
                        low_u(s, 3)
                    if nxt:
                        places(s + 1, 1 - par)
                    if now:
                        for h in range(2):
                            dve.wait_ge(s_ops, s * 2 + (2 * g0 + h + 1))
                            xc = X[:, bass.ds(s * J + 2 * h, 2), :]
                            dve.scalar_tensor_tensor(xc, bank[:, 6 if h == 0 else 0, :].rearrange("p (j d) -> p j d", j=2),
                                                     0.5, xc, ALU.mult, ALU.add).then_inc(s_xout, 1)

                dve.wait_ge(s_wlo, 4 * (layer + 1))
                dve.wait_ge(s_elo, 8)
                for par in range(2):
                    ch.link(dve.memset(rows[:, par, :, D:ROW], 0.0))
                ch.link(dve.tensor_copy(carry[:], cst[:, C_BASE:C_BASE + E]))
                ch.settle()
                run_steps(dve, step, -2, 2, CH - 2, CH, 2, ch, DVE_A)

            def block_table(layer):
                one = slice(0, 1)
                n8, nb, cb = line[:, 0, 0:E], line[:, 1, 0:E], line[:, 2, 0:E]
                ch.settle()
                ch.link(dve.tensor_tensor(n8, carry[one, :], cst[one, C_BASE:C_BASE + E], ALU.subtract))
                ch.link(dve.tensor_copy(table[:, 2 * BLOCKS:2 * BLOCKS + E], carry[one, :]))
                ch.settle()
                ch.link(dve.tensor_tensor(over[:], bc(n8.unsqueeze(2), [1, E, TILES]),
                                          bc(cst[one, C_THR:C_THR + TILES].unsqueeze(1), [1, E, TILES]), ALU.is_gt))
                ch.settle()
                ch.link(dve.tensor_reduce(nb, over[:], AX.X, ALU.add))
                ch.settle()
                ch.link(dve.tensor_tensor_scan(cb, cst[one, C_ONE8:C_ONE8 + E], nb, 0.0, ALU.mult, ALU.add))
                ch.settle()
                blk = cst[one, C_BLK:C_BLK + BLOCKS]
                ch.link(dve.tensor_tensor(past[:, 0], bc(blk.unsqueeze(2), [1, BLOCKS, E]),
                                          bc(cb.unsqueeze(1), [1, BLOCKS, E]), ALU.is_ge))
                ch.settle()
                ch.link(dve.tensor_tensor(past[:, 1], past[:, 0], bc(nb.unsqueeze(1), [1, BLOCKS, E]), ALU.mult))
                ch.settle()
                ch.link(dve.tensor_reduce(line[:, 3:5], past[:], AX.X, ALU.add))
                ch.settle()
                ch.link(dve.tensor_tensor(line[:, 5], blk, line[:, 4], ALU.subtract))
                ch.link(dve.tensor_scalar(table[:, BLOCKS:2 * BLOCKS], line[:, 3], float(E - 1), None, ALU.min))
                ch.settle()
                ch.link(dve.tensor_scalar(line[:, 5], line[:, 5], float(P), None, ALU.mult))
                ch.settle()
                dve.scalar_tensor_tensor(table[:, 0:BLOCKS], line[:, 3], float(CAP), line[:, 5],
                                         ALU.mult, ALU.add).then_inc(s_table, 1)

            def phase_b(layer):
                p0 = PAIRS * layer

                def step(s, u, q):
                    par = u % 2
                    flat = "p k b t -> p (k b t)"
                    if inside(s - 1, PAIRS):
                        dve.wait_ge(s_hh, s + p0)
                        low(HT["l"][:, 1 - par].rearrange(flat), bank[:, 5 - par, :],
                            HT["h"][:, 1 - par].rearrange(flat)).then_inc(s_hl, 1)
                    if inside(s + 1, PAIRS):
                        slot = (u + 1) % 4
                        turn = q if u < 3 else q + 1
                        atleast(dve, s_ysc[slot], turn * 32 + YW * layer)
                        dve.wait_ge(s_bh, s + (p0 + 2))
                        dve.tensor_copy(goal[:, slot, :], XB[:, slot, :, D].bitcast(I32))
                        low(XBT["l"][:, 1 - par].rearrange(flat), bank[:, 1 - par, :],
                            XBT["h"][:, 1 - par].rearrange(flat)).then_inc(s_bl, 1)
                    if inside(s - 1, PAIRS):
                        slot = (u + 3) % 4
                        dve.wait_ge(s_yps, s + p0)
                        dve.tensor_copy(YB[:, slot].rearrange("p b d -> p (b d)"), bank[:, 7 - par, :]).then_inc(s_yok, 1)

                run_steps(dve, step, -1, 4, PAIRS - 4, PAIRS + 1, 4)

            def attention(s, par, half):
                if inside(s + 1, CH):
                    c = s + 1
                    dve.wait_ge(s_yg, c * 32 + 32)
                    for k in range(TOPK):
                        for j in range(J):
                            t = c * J + j
                            xt = X[:, bass.ds(t, 1), :].rearrange("p a d -> p (a d)")
                            ins = dve.scalar_tensor_tensor(xt, YG[:, k, j, :], gates[:, k, bass.ds(t, 1)], xt,
                                                           ALU.mult, ALU.add)
                            if k == 1 and j == J - 1:
                                ins.then_inc(s_comb, 1)
                            else:
                                ch.link(ins)
                        if k == 0:
                            ch.settle()
                    dve.wait_ge(s_comb, c + 1)
                    apart(dve)
                    stats(c, 1 - par)
                if inside(s, CH):
                    dve.wait_ge(s_kev, s * 2 + 2)
                    dve.tensor_tensor(RN[:, 0, :], PR[:, 0, :], PR[:, 1, :], ALU.add).then_inc(s_ksum, 1)
                    dve.wait_ge(s_nps, s + 1)
                    nys, nya = ny[:, 0:24], ny[:, 24:48]
                    by = "p (j w) -> p j w"
                    ch.link(dve.tensor_copy(nys, bank[:, 7, 0:24]))
                    ch.settle()
                    ch.link(dve.scalar_tensor_tensor(nya, nys, -1.0, nys, ALU.mult, ALU.max))
                    if par == 0:
                        ch.link(dve.memset(ny[:, 72:73], 0.0))
                    else:
                        ch.link(dve.tensor_copy(ny[:, 72:73], ny[:, 76:77]))
                    ch.settle()
                    ch.link(dve.tensor_scalar(nya, nya, FFT_EPS, None, ALU.add))
                    ch.settle()
                    ch.link(dve.reciprocal(nya, nya))
                    ch.settle()
                    ch.link(dve.tensor_tensor(nya, nya, nys, ALU.mult))
                    ch.settle()
                    ch.link(dve.tensor_tensor(ny[:, 64:68], nya.rearrange(by, w=6)[:, :, 0],
                                              nys.rearrange(by, w=6)[:, :, 2], ALU.mult))
                    ch.settle()
                    dve.tensor_tensor_scan(ny[:, 73:77], cst[:, C_ONE8:C_ONE8 + J], ny[:, 64:68], ny[:, 72:73],
                                           ALU.mult, ALU.add).then_inc(s_nkv, 1)
                    dve.wait_ge(s_kroot, s + 1)
                    ch.link(dve.tensor_scalar(RN[:, 0, :], RN[:, 0, :], FFT_EPS, None, ALU.add))
                    ch.settle()
                    ch.link(dve.reciprocal(RN[:, 0, :], RN[:, 0, :]))
                    ch.settle()
                    ch.link(dve.tensor_tensor(FK[:], FK[:], bc(RN[:, 0:1, :], [P, 2, N]), ALU.mult))
                    if par == 1:
                        ch.link(dve.tensor_copy(ny[:, 48:50], CUM[:, :, N - 1]))
                    ch.settle()
                    dve.wait_ge(s_vps, s + 1)
                    ch.link(dve.tensor_tensor(PR[:], FK[:], bank[:, 4:6, :], ALU.mult))
                    ch.settle()
                    ch.link(dve.tensor_tensor_scan(CUM[:, 0, :], PR[:, 0, :], PR[:, 1, :],
                                                   ny[:, 48:49] if par == 1 else 0.0, ALU.add, ALU.subtract))
                    ch.settle()
                    ch.link(dve.tensor_tensor(PR[:, 0, :], FK[:, 1, :], bank[:, 4, :], ALU.mult))
                    dve.tensor_tensor(PR[:, 1, :], FK[:, 0, :], bank[:, 5, :], ALU.mult).then_inc(s_vused, 1)
                    dve.wait_ge(s_vused, s + 1)
                    dve.tensor_tensor_scan(CUM[:, 1, :], PR[:, 0, :], PR[:, 1, :],
                                           ny[:, 49:50] if par == 1 else 0.0, ALU.add, ALU.add).then_inc(s_kvd, 1)
                if inside(s + 1, CH):
                    atleast(dve, s_add, s + 1)
                    normalise(s + 1, 1 - par, XN, s + (CH + 2), s_txn)
                if inside(s, CH):
                    dve.wait_ge(s_qev, s + 1)
                    dve.tensor_tensor(RN[:, 1, :], PR[:, 0, :], PR[:, 1, :], ALU.add).then_inc(s_qsum, 1)
                    dve.wait_ge(s_nsum, s + 1)
                    dve.tensor_tensor(ny[:, 80:84], bank[:, 7, 32:36], nya.rearrange(by, w=6)[:, :, 4],
                                      ALU.mult).then_inc(s_npq, 1)
                    dve.wait_ge(s_qroot, s + 1)
                    ch.link(dve.tensor_scalar(RN[:, 1, :], RN[:, 1, :], FFT_EPS, None, ALU.add))
                    ch.settle()
                    ch.link(dve.reciprocal(RN[:, 1, :], RN[:, 1, :]))
                    ch.settle()
                    ch.link(dve.tensor_tensor(FQ[:], FQ[:], bc(RN[:, 1:2, :], [P, 2, N]), ALU.mult))
                    ch.settle()
                if inside(s + 1, CH):
                    dve.wait_ge(s_ah, s + 2)
                    low(XA["l"][:], bank[:, 0:2, :], XA["h"][:]).then_inc(s_al, 1)
                if inside(s, CH):
                    ch.link(dve.tensor_tensor(PR[:], CUM[:], FQ[:], ALU.mult))
                    ch.settle()
                    ch.link(dve.tensor_tensor(KV[:, 0, :], PR[:, 0, :], PR[:, 1, :], ALU.add))
                    ch.settle()
                    ch.link(dve.tensor_tensor(PR[:, 0, :], CUM[:, 1, :], FQ[:, 0, :], ALU.mult))
                    ch.link(dve.tensor_tensor(PR[:, 1, :], CUM[:, 0, :], FQ[:, 1, :], ALU.mult))
                    ch.settle()
                    dve.tensor_tensor(KV[:, 1, :], PR[:, 0, :], PR[:, 1, :], ALU.subtract).then_inc(s_p, 1)
                    dve.wait_ge(s_nh, s + 1)
                    low(PN["l"][:].rearrange("p j t -> p (j t)"), bank[0:1, 5, :],
                        PN["h"][:].rearrange("p j t -> p (j t)")).then_inc(s_nl, 1)
                    dve.wait_ge(s_ph, s + 1)
                    low(VH["l"][:], KV[:], VH["h"][:]).then_inc(s_pl, 1)
                    dve.wait_ge(s_add, s + 1)
                    for h in range(2):
                        dve.wait_ge(s_aps, s * 2 + (h + 1))
                        xc = X[:, bass.ds(s * J + 2 * h, 2), :]
                        dve.tensor_tensor(xc, xc, bank[:, 6 if h == 0 else 4, :].rearrange("p (j d) -> p j d", j=2),
                                          ALU.add).then_inc(s_aout, 1)

            dve.wait_ge(s_const, 32)
            ch.link(dve.tensor_copy(ones_b[:], ones_f))
            ch.link(dve.scalar_tensor_tensor(tri_b[:], tri_f, 1.0, ident, ALU.subtract, ALU.subtract))
            dve.memset(half_neg[:], -0.5).then_inc(s_small, 1)
            shared_weights(0)
            for w in (1, 2):
                raw = raw_ew[w][:].rearrange("p e k n -> p (e k n)")
                for n, i in enumerate(range(0, E * KD * HR, 1024)):
                    dve.wait_ge(s_ehi, 4 * (w - 1) + n + 1)
                    low(EW[w, "l"][:, i:i + 1024], raw[:, i:i + 1024], EW[w, "h"][:, i:i + 1024]).then_inc(s_elo, 1)
            phase_a(0)
            block_table(0)
            phase_b(0)
            dve.wait_ge(s_mhi, 2)
            low(WI["l"][:], raw_inv[:], WI["h"][:]).then_inc(s_mlo, 1)
            for i in range(3):
                for k in range(KD):
                    dve.wait_ge(s_mhi, 2 * i + k + 3)
                    ch.link(low(WF["l"][:, k, i, :], bank[:, 2 * i + k, 0:NW], WF["h"][:, k, i, :]))
            ch.settle()
            dve.nop().then_inc(s_mlo, 2)
            run_steps(dve, attention, -1, 2, CH - 2, CH, 2, ch, DVE_T)
            dve.wait_ge(s_aout, 2 * CH)
            shared_weights(1)
            phase_a(1)
            block_table(1)
            phase_b(1)

            def last(c, par, half):
                dve.wait_ge(s_f[par], half * 32 + 32)
                for k in range(TOPK):
                    for j in range(J):
                        t = c * J + j
                        xt = X[:, bass.ds(t, 1), :].rearrange("p a d -> p (a d)")
                        ins = dve.scalar_tensor_tensor(xt, YF[:, par, k, j, :], gates[:, k, bass.ds(t, 1)], xt,
                                                       ALU.mult, ALU.add)
                        if k == 1 and j == J - 1:
                            ins.then_inc(s_fc, 1)
                        else:
                            ch.link(ins)
                    if k == 0:
                        ch.settle()

            dve.wait_ge(s_xout, 4 * CH)
            run_steps(dve, last, 0, 2, CH, CH, 2, ch, 14)


_INS = ["L0_attn_x", "L0_attn_Wq", "L0_attn_Wk", "L0_attn_Wv", "L0_ffn_router_w", "L0_ffn_router_bias", "L0_ffn_sw1",
        "L0_ffn_sw3", "L0_ffn_sw2", "L0_ffn_ew1", "L0_ffn_ew2"]


def kernel(**inputs):
    import concourse.bacc as bacc
    from concourse.bass_utils import run_bass_kernel_spmd

    nc = bacc.Bacc("TRN2", target_bir_lowering=False, num_devices=1)
    data = {f"in_{n}": np.ascontiguousarray(inputs[n]) for n in _INS}
    data.update({f"in_{n}": a for n, a in constants().items()})
    args = {n: nc.dram_tensor(n, a.shape, mybir.dt.from_np(a.dtype), kind="ExternalInput").ap() for n, a in data.items()}
    out = nc.dram_tensor("out_0", (B, S, D), F32, kind="ExternalOutput").ap()
    build(nc, *(args[f"in_{n}"] for n in _INS), args["in_c_main"], args["in_c_fwd"], args["in_c_inv"], args["in_c_tok"],
          args["in_c_fill"], args["in_c_sign"], out)
    return run_bass_kernel_spmd(nc, [data], core_ids=[0]).results[0]["out_0"]
```

```python
from contextlib import ExitStack

import numpy as np

import concourse.bass as bass
from concourse import mybir

F32 = mybir.dt.float32
F32R = mybir.dt.float32r
BF16 = mybir.dt.bfloat16
I32 = mybir.dt.int32
ALU = mybir.AluOpType
ACT = mybir.ActivationFunctionType
AX = mybir.AxisListType

P = 128
B, S, D = 8, 1024, 256
TOKENS = B * S
TILES = TOKENS // P
J = 4
CH = TILES // J
N = J * P
KD = D // P
FS = 512
M = FS // P
E, TOPK = 8, 2
HR = 256
CAP = TOKENS + P
ROW = D + 8
BLOCKS = TOPK * TILES + E
PAIRS = BLOCKS // 2
LN_EPS, FFT_EPS, GATE_EPS = 1e-5, 1e-8, 1e-9
NF = D // 2
NW = D + 2

DVE_A, DVE_T = 84, 57

C_ID, C_TRI, C_ONE, C_RESE, C_RESJ = 0, 128, 256, 384, 416
C_BASE, C_ONE8, C_THR, C_BLK, C_END = 448, 456, 464, 528, 528 + BLOCKS


def constants():
    c = np.zeros((P, C_END), np.float32)
    p = np.arange(P)
    c[:, C_ID:C_ID + P] = np.eye(P)
    c[:, C_TRI:C_TRI + P] = p[:, None] <= p[None, :]
    c[:, C_ONE:C_ONE + P] = 1.0
    c[:, C_RESE:C_RESE + J * E] = (np.arange(J * E) % E != 0)
    c[:, C_RESJ:C_RESJ + J * E] = (np.arange(J * E) % J != 0)
    c[:, C_BASE:C_BASE + E] = np.arange(E) * CAP
    c[:, C_ONE8:C_ONE8 + E] = 1.0
    c[:, C_THR:C_THR + TILES] = np.arange(TILES) * P
    c[:, C_BLK:C_BLK + BLOCKS] = np.arange(BLOCKS)
    n = np.arange(D)[:, None].astype(np.float64)
    f = np.arange(NF)[None, :].astype(np.float64)
    ang = 2.0 * np.pi * n * f / D
    fwd = np.zeros((D, NW), np.float32)
    fwd[:, :NF] = np.cos(ang)
    fwd[:, NF:D] = -np.sin(ang)
    fwd[:, D] = 1.0 - 2.0 * (np.arange(D) % 2)
    w = np.full((NF, 1), 2.0 / D)
    w[0] = 1.0 / D
    inv = np.concatenate([w * np.cos(ang.T), -w * np.sin(ang.T)]).astype(np.float32)
    tok = np.zeros((P, TOPK, TILES), np.int32)
    tok[:, 0] = p[:, None] + P * np.arange(TILES)[None, :]
    tok[:, 1] = tok[:, 0] + TOKENS
    fill = np.zeros((2 * E * P, ROW), np.int32)
    fill[:, D] = 2 * TOKENS + np.arange(2 * E * P)
    sign = ((1.0 - 2.0 * (np.arange(D) % 2)) / D).astype(np.float32).reshape(1, D)
    return {"c_main": c, "c_sign": sign, "c_fwd": fwd, "c_inv": inv, "c_tok": tok.reshape(P, 2 * TILES), "c_fill": fill}


class Tally:

    def __init__(self, eng, sem):
        self.eng, self.sem, self.n, self.reg = eng, sem, 0, 0

    def link(self, ins):
        self.n += 1
        ins.then_inc(self.sem, 1)

    def settle(self):
        self.eng.wait_ge(self.sem, self.reg + self.n)


def run_steps(eng, step, lo, a, b, hi, unroll, tally=None, per_turn=0):
    for s in range(lo, a):
        step(s, s % unroll, s // unroll)
    n0 = tally.n if tally else 0
    with eng.Fori(0, (b - a) // unroll) as i:
        if tally:
            tally.reg = i * per_turn
        for u in range(unroll):
            step(i * unroll + (a + u), (a + u) % unroll, i + a // unroll)
    if tally:
        assert tally.n - n0 == per_turn, (tally.n - n0, per_turn)
        tally.reg = 0
        tally.n = n0 + per_turn * ((b - a) // unroll)
    for s in range(b, hi):
        step(s, s % unroll, s // unroll)


def inside(c, n):
    return not isinstance(c, int) or 0 <= c < n


def atleast(eng, sem, value):
    if not isinstance(value, int) or value > 0:
        eng.wait_ge(sem, value)


def build(nc, x, wq, wk, wv, rw, rb, sw1, sw3, sw2, ew1, ew2, c_main, c_fwd, c_inv, c_tok, c_fill, c_sign, out):
    ctx = ExitStack()
    with ctx:
        def sb(name, shape, dt):
            return ctx.enter_context(nc.sbuf_tensor(name, shape, dt))

        def sem(name):
            return ctx.enter_context(nc.semaphore(name))

        lists = nc.dram_tensor("lists", (E * CAP + E * P, ROW), F32, kind="Internal").ap()
        results = nc.dram_tensor("results", (2 * TOKENS + 2 * E * P, D), F32, kind="Internal").ap()

        X = sb("X", [P, TILES, D], F32)
        EW = {(w, h): sb(f"ew{w}_{h}", [P, E * KD * HR], F32R) for w in (1, 2) for h in "hl"}
        gates = sb("gates", [P, 2, TILES], F32)
        cst = sb("cst", [P, C_END], F32)
        tok = sb("tok", [P, 2 * TILES], I32)
        tri_b = sb("tri_b", [P, P], BF16)
        ones_b = sb("ones_b", [P, P], BF16)
        carry = sb("carry", [P, E], F32)
        table = sb("table", [1, 2 * BLOCKS + E], I32)
        st = sb("st", [P, 2, J, 6], F32)
        mv = sb("mv", [P, 2, J, 2], F32)
        rstd = sb("rstd", [P, 2, J], F32)
        shift = sb("shift", [P, 2, J], F32)
        neg_one = sb("neg_one", [P, J], F32)
        half_neg = sb("half_neg", [P, J], F32)
        bias_r = sb("bias_r", [P, J, E], F32)
        ident = cst[:, C_ID:C_ID + P]
        tri_f = cst[:, C_TRI:C_TRI + P]
        ones_f = cst[:, C_ONE:C_ONE + P]

        region_at = (nc.sbuf_base + 31) // 32 * 32
        region_size = (nc.sbuf_usable_end - region_at) // 32 * 32 - 32
        sb("region", [P, region_size], mybir.dt.uint8)
        cursor = {}

        def place(phase, name, shape, dt, at=None):
            size = int(np.prod(shape[1:])) * (2 if dt == BF16 else 4)
            if at is None:
                at = cursor.get(phase, 0)
                cursor[phase] = (at + size + 31) // 32 * 32
            where[name] = at
            assert at + size <= region_size, (phase, name, at + size, region_size)
            return nc.alloc_sbuf_tensor_at(f"{phase}_{name}", shape, dt, offset=region_at + at)

        where = {}
        SW = {(w, h): place("a", f"sw{w}{h}", [P, 2 * FS], F32R) for w in (1, 3, 2) for h in "hl"}
        RW = {h: place("a", f"rw{h}", [P, KD, E], F32R) for h in "hl"}
        rows = place("a", "rows", [P, 2, J, ROW], F32)
        XT = {h: place("a", f"xt{h}", [P, 2, KD, N], F32R) for h in "hl"}
        U = {h: place("a", f"u{h}", [P, M, N], F32R) for h in "hl"}
        gate_u = place("a", "gate_u", [P, 2, N], F32)
        prob = place("a", "prob", [P, J, E], F32)
        small = place("a", "small", [P, 15, J, E], F32)
        slots = place("a", "slots", [P, 2, 2, J], I32)
        inc_b = place("a", "inc_b", [P, 2, E, J], BF16)
        raw_sw = {1: place("w", "raw_sw1", [P, 2 * FS], F32, where["rows"]),
                  3: place("w", "raw_sw3", [P, 2 * FS], F32, where["rows"] + 4 * 2 * FS),
                  2: place("w", "raw_sw2", [P, 2 * FS], F32, where["gate_u"])}
        raw_rw = place("w", "raw_rw", [E, D], F32, where["small"])
        raw_rb = place("w", "raw_rb", [1, J, E], F32, where["small"] + 4 * D)
        raw_ew = {1: place("w", "raw_ew1", [P, E, KD, HR], F32, where["xth"]),
                  2: place("w", "raw_ew2", [P, E, KD, HR], F32, where["uh"])}
        XB = place("b", "xb", [P, 4, 2, ROW], F32)
        XBT = {h: place("b", f"xbt{h}", [P, 2, KD, 2, P], F32R) for h in "hl"}
        HB = place("b", "hb", [P, 2, 2, HR], F32)
        HT = {h: place("b", f"ht{h}", [P, 2, KD, 2, P], F32R) for h in "hl"}
        YB = place("b", "yb", [P, 4, 2, D], F32)
        goal = place("b", "goal", [P, 4, 2], I32)
        over = place("b", "over", [1, E, TILES], F32)
        past = place("b", "past", [1, 2, BLOCKS, E], F32)
        line = place("b", "line", [1, 6, BLOCKS], F32)
        WF = {h: place("t", f"wf{h}", [P, KD, 3, NW], F32R) for h in "hl"}
        WI = {h: place("t", f"wi{h}", [P, 2, D], F32R) for h in "hl"}
        sign = place("t", "sign", [1, D], F32R)
        YG = place("t", "yg", [P, 2, J, D], F32)
        XN = place("t", "xn", [P, J, D], F32)
        XA = {h: place("t", f"xa{h}", [P, KD, N], F32R) for h in "hl"}
        FK = place("t", "fk", [P, 2, N], F32)
        PR = place("t", "pr", [P, 2, N], F32)
        FQ = place("t", "fq", [P, 2, N], F32)
        RN = place("t", "rn", [P, 2, N], F32)
        CUM = place("t", "cum", [P, 2, N], F32)
        ny = place("t", "ny", [P, 96], F32)
        PN = {h: place("t", f"pn{h}", [1, J, P], F32R) for h in "hl"}
        PQ = place("t", "pq", [P, 2, N], F32)
        PS = place("t", "ps", [P, 2, N], F32, where["rn"])
        KV = place("t", "kv", [P, 2, N], F32, where["fq"])
        VH = {h: place("t", f"vh{h}", [P, 2, N], F32R) for h in "hl"}
        raw_w = [place("t", f"raw_w{i}", [P, KD, D], F32, where["yg"] + i * 4 * KD * D) for i in range(3)]
        raw_fwd = place("t", "raw_fwd", [P, KD, NW], F32, where["xn"])
        raw_inv = place("t", "raw_inv", [P, 2, D], F32, where["yg"] + 3 * 4 * KD * D)
        raw_sign = place("t", "raw_sign", [1, D], F32, where["xn"] + 4 * KD * NW + 16)
        YF = place("f", "yf", [P, 4, 2, J, D], F32)

        bank = ctx.enter_context(nc.psum_tensor("bank", [P, 8, 512], F32))

        def apart(eng):
            eng.sem_inc(s_passed, 1)

        s_passed = sem("passed")

        s_const, s_small, s_raw, s_raw_e = sem("const_in"), sem("small_ok"), sem("raw_in"), [sem("raw_e1"), sem("raw_e2")]
        s_whi, s_wlo, s_ehi, s_elo, s_rps = sem("w_hi"), sem("w_lo"), sem("e_hi"), sem("e_lo"), sem("router_w_ps")
        s_spare, s_mat, s_mps, s_mhi, s_mlo = sem("spare_rows"), sem("mat_in"), sem("mat_ps"), sem("mat_hi"), sem("mat_lo")
        s_x = [sem("x_in0"), sem("x_in1")]
        s_var, s_rstd = sem("var_ok"), sem("rstd_ok")
        s_xn, s_tps, s_xh, s_xl = sem("xn_ok"), sem("xt_ps"), sem("xt_h"), sem("xt_l")
        s_logit, s_prob, s_mask, s_rank, s_slot = (sem("logits"), sem("prob_ok"), sem("mask_ok"), sem("rank_ps"),
                                                   sem("slots_ok"))
        s_hps, s_sig, s_u, s_uh, s_ul = sem("h_ps"), sem("sig_ok"), sem("u_ok"), sem("u_hi"), sem("u_lo")
        s_ops, s_xout, s_scat, s_gated = sem("o_ps"), sem("x_out"), sem("scattered"), sem("gates_ok")
        s_table, s_tail = sem("table_ok"), sem("tail_rows")
        s_xb = [sem(f"xb_in{i}") for i in range(4)]
        s_bps, s_bh, s_bl, s_mm1, s_gelu = sem("xb_ps"), sem("xb_h"), sem("xb_l"), sem("h1_ps"), sem("gelu_ok")
        s_hT, s_hh, s_hl, s_yps, s_yok = sem("ht_ps"), sem("ht_h"), sem("ht_l"), sem("y_ps"), sem("y_ok")
        s_ysc = [sem(f"y_out{i}") for i in range(4)]
        s_yg, s_comb, s_txn, s_add, s_atp, s_ah, s_al = (sem("yg_in"), sem("combined"), sem("a_xn"), sem("a_added"),
                                                         sem("a_xt_ps"), sem("a_xt_h"), sem("a_xt_l"))
        s_kps, s_vps, s_nps, s_qps = sem("k_ps"), sem("v_ps"), sem("nyq_ps"), sem("q_ps")
        s_kev, s_ksum, s_kroot, s_vused, s_kvd = sem("k_out"), sem("k_sum"), sem("k_root"), sem("v_used"), sem("kv_done")
        s_qc, s_qev, s_qsum, s_qroot, s_p, s_ph, s_pl = (sem("q_copy"), sem("q_out"), sem("q_sum"), sem("q_root"),
                                                         sem("p_ok"), sem("p_h"), sem("p_l"))
        s_nkv, s_nsum, s_npq, s_nt, s_nh, s_nl = (sem("nyq_kv"), sem("nyq_sum"), sem("nyq_pq"), sem("nyq_t"),
                                                  sem("nyq_h"), sem("nyq_l"))
        s_qinv, s_qn, s_ps, s_aps, s_aout = sem("q_inverse"), sem("q_norm"), sem("ps_ok"), sem("a_ps"), sem("a_out")
        s_f = [sem(f"f_in{i}") for i in range(4)]
        s_fc, s_store = sem("f_combined"), sem("stored")
        s_dve, s_pool = sem("dve_chain"), sem("pool_chain")

        x_d = x.rearrange("b s d -> (b s) d").rearrange("(t p) d -> p t d", p=P)
        out_d = out.rearrange("b s d -> (b s) d").rearrange("(t p) d -> p t d", p=P)
        res_d = results[0:2 * TOKENS, :].rearrange("(k t p) d -> p k t d", p=P, k=2)
        YW = PAIRS // 4 * 32

        block = ctx.enter_context(nc.Block())

        @block.sync
        def _(sp):
            sp.dma_start(cst[:], c_main).then_inc(s_const, 16)
            sp.dma_start(tok[:], c_tok).then_inc(s_const, 16)

            def shared_weights():
                sp.dma_start(raw_rw[:], rw).then_inc(s_raw, 16)
                for j in range(J):
                    sp.dma_start(raw_rb[:, j, :], rb.rearrange("(a e) -> a e", a=1)).then_inc(s_raw, 16)
                for w, src in ((1, sw1), (3, sw3), (2, sw2)):
                    k = KD if w != 2 else M
                    sp.dma_start(raw_sw[w][:].rearrange("p (k n) -> p k n", k=k),
                                 src.rearrange("(k p) n -> p k n", p=P)).then_inc(s_raw, 16)

            shared_weights()
            for i, src in enumerate((ew1, ew2)):
                sp.dma_start(raw_ew[i + 1][:].rearrange("p e k n -> p (e k) n"),
                             src.rearrange("e (k p) n -> p (e k) n", p=P)).then_inc(s_raw_e[i], 16)
            fill = c_fill.bitcast(F32)
            sp.dma_start(lists[E * CAP:E * CAP + E * P, :], fill[E * P:2 * E * P, :]).then_inc(s_spare, 16)

            def load_x(c, par, half):
                atleast(sp, s_x[par], half * 16)
                sp.dma_start(X[:, bass.ds(c * J, J), :], x_d[:, bass.ds(c * J, J), :]).then_inc(s_x[par], 16)

            run_steps(sp, load_x, 0, 2, CH, CH, 2)

            def phase_b(layer):
                sp.wait_ge(s_table, layer + 1)
                for e in range(E):
                    end = sp.value_load(table[0:1, 2 * BLOCKS + e:2 * BLOCKS + e + 1], min_val=e * CAP,
                                        max_val=e * CAP + TOKENS)
                    sp.dma_start(lists[bass.ds(end, P), :], fill[e * P:(e + 1) * P, :]).then_inc(s_tail, 16)
                sp.wait_ge(s_tail, E * 16 * (layer + 1))
                sp.wait_ge(s_spare, 16)
                sp.wait_ge(s_scat, 2 * J * 16 * CH * (layer + 1))
                p0 = PAIRS * layer

                def step(n, slot, q):
                    atleast(sp, s_bl, n + (p0 - 3) if not isinstance(n, int) or n >= 4 else 0)
                    for blk in range(2):
                        row = sp.value_load(table[0:1, bass.ds(n * 2 + blk, 1)], min_val=0,
                                            max_val=E * CAP + (E - 1) * P)
                        sp.dma_start(XB[:, slot, blk, :], lists[bass.ds(row, P), :]).then_inc(s_xb[slot], 16)

                run_steps(sp, step, 0, 4, PAIRS, PAIRS, 4)

            def results_in(layer):
                for i in range(4):
                    sp.wait_ge(s_ysc[i], YW * (layer + 1))

            phase_b(0)
            results_in(0)
            for i, src in enumerate((wk, wv, wq)):
                sp.dma_start(raw_w[i][:], src.rearrange("(k p) n -> p k n", p=P)).then_inc(s_mat, 16)
            sp.dma_start(raw_fwd[:], c_fwd.rearrange("(k p) n -> p k n", p=P)).then_inc(s_mat, 16)
            sp.dma_start(raw_inv[:], c_inv.rearrange("(k p) n -> p k n", p=P)).then_inc(s_mat, 16)
            sp.dma_start(raw_sign[:], c_sign).then_inc(s_mat, 16)
            sp.wait_ge(s_mlo, 3)

            def load_results(c, par, half):
                atleast(sp, s_comb, c)
                for k in range(2):
                    sp.dma_start(YG[:, k, :, :], res_d[:, k, bass.ds(c * J, J), :]).then_inc(s_yg, 16)

            run_steps(sp, load_results, 0, 2, CH, CH, 2)
            sp.wait_ge(s_aout, 2 * CH)
            shared_weights()
            phase_b(1)
            results_in(1)
            def load_last(c, slot, q):
                atleast(sp, s_fc, c - 3)
                for k in range(2):
                    sp.dma_start(YF[:, slot, k, :, :], res_d[:, k, bass.ds(c * J, J), :]).then_inc(s_f[slot], 16)

            sp.wait_ge(s_yok, 2 * PAIRS)
            run_steps(sp, load_last, 0, 4, CH, CH, 4)
            sp.wait_ge(s_store, 16 * CH)

        @block.gpsimd
        def _(pool):
            ch = Tally(pool, s_pool)

            def rstd_of(q, count):
                pool.wait_ge(s_var, count)
                apart(pool)
                ch.link(pool.tensor_scalar(rstd[:, q, :], mv[:, q, :, 1], LN_EPS, 1.0, ALU.add, ALU.mult))
                ch.link(pool.tensor_tensor(shift[:, q, :], mv[:, q, :, 0], neg_one[:], ALU.mult))
                ch.settle()
                ch.link(pool.tensor_tensor(rstd[:, q, :], rstd[:, q, :], half_neg[:, :], ALU.pow))
                ch.settle()
                pool.tensor_tensor(shift[:, q, :], shift[:, q, :], rstd[:, q, :], ALU.mult).then_inc(s_rstd, 1)

            def phase_a(layer):
                g0, v0 = CH * layer, 2 * CH * layer

                def step(s, par, half):
                    if inside(s + 3, CH):
                        rstd_of(1 - par, s + (v0 + 4))
                    if inside(s + 1, CH):
                        c, g, q = s + 1, s + (g0 + 1), 1 - par
                        pool.wait_ge(s_slot, g + 1)
                        for k in range(TOPK):
                            atleast(pool, s_scat, g * 128 + 64 * k)
                            ch.link(pool.tensor_copy(rows[:, q, :, D:D + 1].bitcast(I32),
                                                     tok[:, bass.ds(c * J + k * TILES, J)].unsqueeze(2)))
                            ch.settle()
                            apart(pool)
                            for j in range(J):
                                pool.indirect_dma_start(
                                    out=lists, out_offset=bass.IndirectOffsetOnAxis(ap=slots[:, q, k, j:j + 1], axis=0),
                                    in_=rows[:, q, j, :], in_offset=None).then_inc(s_scat, 16)

                run_steps(pool, step, -3, 2, CH - 4, CH, 2, ch, 10)

            def phase_b(layer):
                def step(n, slot, q):
                    pool.wait_ge(s_yok, n + (PAIRS * layer + 1))
                    apart(pool)
                    for blk in range(2):
                        pool.indirect_dma_start(
                            out=results,
                            out_offset=bass.IndirectOffsetOnAxis(ap=goal[:, slot, blk:blk + 1], axis=0),
                            in_=YB[:, slot, blk, :], in_offset=None).then_inc(s_ysc[slot], 16)

                run_steps(pool, step, 0, 4, PAIRS, PAIRS, 4)

            pool.wait_ge(s_small, 1)
            phase_a(0)
            phase_b(0)

            def attention(s, par, half):
                now, nxt = inside(s, CH), inside(s + 1, CH)
                if now:
                    pool.wait_ge(s_kev, s * 2 + 2)
                    atleast(pool, s_p, s)
                    pool.tensor_tensor(RN[:, 0, :], PR[:, 0, :], PR[:, 1, :], ALU.add).then_inc(s_ksum, 1)
                    pool.wait_ge(s_qev, s + 1)
                    pool.tensor_tensor(RN[:, 1, :], PQ[:, 0, :], PQ[:, 1, :], ALU.add).then_inc(s_qsum, 1)
                if nxt:
                    rstd_of(1 - par, s + (CH + 2))
                    pool.wait_ge(s_txn, s + 2)
                    xc = X[:, bass.ds((s + 1) * J, J), :]
                    pool.tensor_tensor(xc, xc, XN[:], ALU.add).then_inc(s_add, 1)
                if now:
                    pool.wait_ge(s_qinv, s + 1)
                    pool.tensor_tensor(FQ[:], FQ[:], RN[:, 1:2, :].to_broadcast([P, 2, N]), ALU.mult).then_inc(s_qn, 1)
                    pool.wait_ge(s_qn, s + 1)
                    pool.wait_ge(s_kvd, s + 1)
                    pool.tensor_tensor(PS[:, 1, :], CUM[:, 0, :], FQ[:, 1, :], ALU.mult).then_inc(s_ps, 1)

            run_steps(pool, attention, -1, 2, CH - 2, CH, 2, ch, 6)
            phase_a(1)
            phase_b(1)

        @block.scalar
        def _(act):
            def copy(o, i):
                return act.activation(o, i, ACT.Copy)

            def shared_weights(layer):
                act.wait_ge(s_raw, 128 * (layer + 1))
                for w in (1, 3, 2):
                    copy(SW[w, "h"][:], raw_sw[w][:]).then_inc(s_whi, 1)
                act.wait_ge(s_rps, 2 * layer + 1)
                copy(RW["h"][:], bank[:, 7, 0:KD * E].rearrange("p (k e) -> p k e", k=KD)).then_inc(s_whi, 1)

            def phase_a(layer):
                g0, v0 = CH * layer, 2 * CH * layer

                def sigmoid_gate(s, m):
                    n = s * M + (g0 * M + m)
                    act.wait_ge(s_hps, n + 1)
                    atleast(act, s_ul, n - 1)
                    act.activation(gate_u[:, m % 2, :], bank[:, 2 + 2 * (m % 2), :], ACT.Sigmoid).then_inc(s_sig, 1)

                def high_u(s, m):
                    n = s * M + (g0 * M + m)
                    act.wait_ge(s_u, n + 1)
                    if m == 0:
                        atleast(act, s_ops, s * 2 + 2 * g0)
                    copy(U["h"][:, m, :], gate_u[:, m % 2, :]).then_inc(s_uh, 1)

                def step(s, par, half):
                    now, nxt, far = inside(s, CH), inside(s + 1, CH), inside(s + 2, CH)
                    if now:
                        high_u(s, 0)
                        high_u(s, 1)
                        sigmoid_gate(s, 2)
                        high_u(s, 2)
                    if nxt:
                        act.wait_ge(s_logit, s + (g0 + 2))
                        atleast(act, s_gated, s + (g0 + 1))
                        act.activation(prob[:].rearrange("p j e -> p (j e)"), bank[:, 7, 0:J * E],
                                       ACT.Sigmoid).then_inc(s_prob, 1)
                    if now:
                        sigmoid_gate(s, 3)
                    if far:
                        act.wait_ge(s_rstd, s + (v0 + 3))
                        atleast(act, s_scat, s * 128 + 128 * (g0 + 1) if now else 128 * g0)
                        for j in range(J):
                            ins = act.activation(rows[:, par, j, 0:D],
                                                 X[:, bass.ds((s + 2) * J + j, 1), :].rearrange("p a d -> p (a d)"),
                                                 ACT.Identity, bias=shift[:, par, j:j + 1], scale=rstd[:, par, j:j + 1])
                        ins.then_inc(s_xn, 1)
                    if now:
                        high_u(s, 3)
                    if nxt:
                        sigmoid_gate(s + 1, 0)
                        sigmoid_gate(s + 1, 1)
                    if far:
                        act.wait_ge(s_tps, s + (g0 + 3))
                        copy(XT["h"][:, par, :, :], bank[:, 0:2, :]).then_inc(s_xh, 1)

                act.wait_ge(s_wlo, 4 * (layer + 1))
                act.wait_ge(s_elo, 8)
                run_steps(act, step, -2, 2, CH - 2, CH, 2)

            def expert_weights():
                for w in (1, 2):
                    act.wait_ge(s_raw_e[w - 1], 16)
                    raw = raw_ew[w][:].rearrange("p e k n -> p (e k n)")
                    for i in range(0, E * KD * HR, 1024):
                        copy(EW[w, "h"][:, i:i + 1024], raw[:, i:i + 1024]).then_inc(s_ehi, 1)

            def phase_b(layer):
                p0 = PAIRS * layer

                def step(s, u, q):
                    par = u % 2
                    if inside(s - 1, PAIRS):
                        act.wait_ge(s_hT, s + p0)
                        copy(HT["h"][:, 1 - par].rearrange("p k b t -> p (k b t)"),
                             bank[:, 4 + 1 - par, :]).then_inc(s_hh, 1)
                    if inside(s + 1, PAIRS):
                        act.wait_ge(s_bps, s + (p0 + 2))
                        copy(XBT["h"][:, 1 - par].rearrange("p k b t -> p (k b t)"),
                             bank[:, 1 - par, :]).then_inc(s_bh, 1)
                    if inside(s, PAIRS):
                        act.wait_ge(s_mm1, s + (p0 + 1))
                        act.activation(HB[:, par].rearrange("p b n -> p (b n)"), bank[:, 2 + par, :],
                                       ACT.Gelu).then_inc(s_gelu, 1)

                run_steps(act, step, -1, 4, PAIRS - 4, PAIRS + 1, 4)

            def attention(s, par, half):
                now, nxt = inside(s, CH), inside(s + 1, CH)
                if now:
                    act.wait_ge(s_ksum, s + 1)
                    act.activation(RN[:, 0, :], RN[:, 0, :], ACT.Sqrt).then_inc(s_kroot, 1)
                if nxt:
                    act.wait_ge(s_rstd, s + (CH + 2))
                    atleast(act, s_add, s + 1)
                    atleast(act, s_atp, s + 1)
                    for j in range(J):
                        ins = act.activation(XN[:, j, :],
                                             X[:, bass.ds((s + 1) * J + j, 1), :].rearrange("p a d -> p (a d)"),
                                             ACT.Identity, bias=shift[:, 1 - par, j:j + 1],
                                             scale=rstd[:, 1 - par, j:j + 1])
                    ins.then_inc(s_txn, 1)
                if now:
                    act.wait_ge(s_qsum, s + 1)
                    act.activation(RN[:, 1, :], RN[:, 1, :], ACT.Sqrt).then_inc(s_qroot, 1)
                if nxt:
                    act.wait_ge(s_atp, s + 2)
                    atleast(act, s_qps, s + 1)
                    copy(XA["h"][:], bank[:, 0:2, :]).then_inc(s_ah, 1)
                    act.wait_ge(s_kps, s + 2)
                    atleast(act, s_kvd, s + 1)
                    copy(FK[:], bank[:, 2:4, :]).then_inc(s_kev, 1)
                    act.activation(PR[:], bank[:, 2:4, :], ACT.Square).then_inc(s_kev, 1)
                if now:
                    act.wait_ge(s_p, s + 1)
                    atleast(act, s_aps, s * 2)
                    copy(VH["h"][:], KV[:]).then_inc(s_ph, 1)
                    act.wait_ge(s_nt, s + 1)
                    copy(PN["h"][:].rearrange("p j t -> p (j t)"), bank[0:1, 1, :]).then_inc(s_nh, 1)
                if nxt:
                    act.wait_ge(s_qps, s + 2)
                    atleast(act, s_pl, s + 1)
                    copy(FQ[:], bank[:, 2:4, :]).then_inc(s_qc, 1)
                    act.activation(PQ[:], bank[:, 2:4, :], ACT.Square).then_inc(s_qev, 1)

            shared_weights(0)
            expert_weights()
            phase_a(0)
            phase_b(0)
            act.wait_ge(s_mat, 96)
            copy(WI["h"][:], raw_inv[:]).then_inc(s_mhi, 1)
            copy(sign[:], raw_sign[:]).then_inc(s_mhi, 1)
            for i in range(3):
                for k in range(KD):
                    act.wait_ge(s_mps, 2 * i + k + 1)
                    copy(WF["h"][:, k, i, :], bank[:, 2 * i + k, 0:NW]).then_inc(s_mhi, 1)
            run_steps(act, attention, -1, 2, CH - 2, CH, 2)
            shared_weights(1)
            phase_a(1)
            phase_b(1)

            def store(c, par, half):
                act.wait_ge(s_fc, c + 1)
                act.dma_start(out_d[:, bass.ds(c * J, J), :], X[:, bass.ds(c * J, J), :]).then_inc(s_store, 16)

            run_steps(act, store, 0, 2, CH, CH, 2)

        @block.tensor
        def _(pe):
            def three(o, a, b, first, last):
                pe.matmul(o, a("h"), b("h"), start=first, stop=False)
                pe.matmul(o, a("h"), b("l"), start=False, stop=False)
                return pe.matmul(o, a("l"), b("h"), start=False, stop=last)

            def shared_weights(layer):
                pe.wait_ge(s_raw, 128 * (layer + 1))
                pe.wait_ge(s_const, 32)
                for k in range(KD):
                    ins = pe.transpose(bank[:, 7, k * E:(k + 1) * E], raw_rw[:, k * P:(k + 1) * P], ident[0:E, 0:E])
                ins.then_inc(s_rps, 1)
                if layer == 0:
                    pe.matmul(bank[:, 6, 0:J * E], ones_f[0:1, :], raw_rb[:].rearrange("p j e -> p (j e)"),
                              start=True, stop=True).then_inc(s_rps, 1)

            def phase_a(layer):
                g0 = CH * layer

                def transposes(c, par):
                    g = c + g0
                    pe.wait_ge(s_xn, g + 1)
                    atleast(pe, s_xl, g)
                    atleast(pe, s_xout, (g - 2) * 2)
                    for k in range(KD):
                        for j in range(J):
                            ins = pe.transpose(bank[:, k, j * P:(j + 1) * P], rows[:, par, j, k * P:(k + 1) * P], ident)
                    ins.then_inc(s_tps, 1)

                def router(c, par):
                    g = c + g0
                    pe.wait_ge(s_xl, g + 1)
                    atleast(pe, s_slot, g)
                    for j in range(J):
                        for k in range(KD):
                            ins = three(bank[:, 7, j * E:(j + 1) * E], lambda h: XT[h][:, par, k, j * P:(j + 1) * P],
                                        lambda h: RW[h][:, k, :], k == 0, k == KD - 1)
                    ins.then_inc(s_logit, 1)

                def ranks(c, par):
                    g = c + g0
                    pe.wait_ge(s_mask, g + 1)
                    pe.matmul(bank[:, 7, 64:64 + J * E], tri_b[:], inc_b[:, 0].rearrange("p e j -> p (e j)"),
                              start=True, stop=False)
                    pe.matmul(bank[:, 7, 64:64 + J * E], ones_b[:], inc_b[:, 1].rearrange("p e j -> p (e j)"),
                              start=False, stop=True)
                    pe.matmul(bank[:, 7, 128:128 + E], ones_b[:], inc_b[:, 1, :, J - 1], start=True,
                              stop=True).then_inc(s_rank, 1)

                def hidden(c, par, m):
                    n = c * M + (g0 * M + m)
                    atleast(pe, s_u, n - 1)
                    for w, o in ((1, 2 + 2 * (m % 2)), (3, 3 + 2 * (m % 2))):
                        for k in range(KD):
                            ins = three(bank[:, o, :], lambda h: SW[w, h][:, k * FS + m * P:k * FS + (m + 1) * P],
                                        lambda h: XT[h][:, par, k, :], k == 0, k == KD - 1)
                    ins.then_inc(s_hps, 1)

                def down(c, par, half):
                    g = c + g0
                    if half == 0:
                        pe.wait_ge(s_ul, g * M + M)
                        atleast(pe, s_xout, g * 2)
                    elif inside(c + 2, CH):
                        pe.wait_ge(s_xl, g + 3)
                    for i in range(2):
                        j = 2 * half + i
                        for m in range(M):
                            ins = three(bank[:, 6 if half == 0 else 0, i * D:(i + 1) * D],
                                        lambda h: U[h][:, m, j * P:(j + 1) * P],
                                        lambda h: SW[2, h][:, m * D:(m + 1) * D], m == 0, m == M - 1)
                    ins.then_inc(s_ops, 1)

                def step(s, par, half):
                    now, nxt, far = inside(s, CH), inside(s + 1, CH), inside(s + 2, CH)
                    if now:
                        hidden(s, par, 2)
                    if nxt:
                        router(s + 1, 1 - par)
                    if now:
                        hidden(s, par, 3)
                    if nxt:
                        hidden(s + 1, 1 - par, 0)
                        ranks(s + 1, 1 - par)
                        hidden(s + 1, 1 - par, 1)
                    if far:
                        transposes(s + 2, par)
                    if now:
                        down(s, par, 0)
                        down(s, par, 1)

                pe.wait_ge(s_wlo, 4 * (layer + 1))
                run_steps(pe, step, -2, 2, CH - 2, CH, 2)

            def phase_b(layer):
                p0 = PAIRS * layer

                def load_experts(s, par):
                    for blk in range(2):
                        pe.reg_load(offset[par][blk], table[0:1, bass.ds(s * 2 + (BLOCKS + blk), 1)])

                def weights_at(par):
                    return [pe.snap(offset[par][blk], min_val=0, max_val=E - 1) for blk in range(2)]

                def expert(w, h, e, k):
                    v = EW[w, h][:].rearrange("p (e n) -> p e n", e=E)
                    return v[:, bass.ds(e, 1), k * HR:(k + 1) * HR].rearrange("p a n -> p (a n)")

                def step(s, u, q):
                    par = u % 2
                    if inside(s - 1, PAIRS):
                        pe.wait_ge(s_gelu, s + p0)
                        atleast(pe, s_hl, s + (p0 - 2))
                        for k in range(KD):
                            for blk in range(2):
                                ins = pe.transpose(bank[:, 5 - par, (2 * k + blk) * P:(2 * k + blk + 1) * P],
                                                   HB[:, 1 - par, blk, k * P:(k + 1) * P], ident)
                        ins.then_inc(s_hT, 1)
                    if inside(s + 1, PAIRS):
                        slot = (u + 1) % 4
                        turn = q if u < 3 else q + 1
                        pe.wait_ge(s_xb[slot], turn * 32 + (YW * layer + 32))
                        atleast(pe, s_bl, s + p0)
                        for k in range(KD):
                            for blk in range(2):
                                ins = pe.transpose(bank[:, 1 - par, (2 * k + blk) * P:(2 * k + blk + 1) * P],
                                                   XB[:, slot, blk, k * P:(k + 1) * P], ident)
                        ins.then_inc(s_bps, 1)
                    if inside(s - 1, PAIRS):
                        before = weights_at(1 - par)
                    if inside(s, PAIRS):
                        at = weights_at(par)
                        pe.wait_ge(s_bl, s + (p0 + 1))
                        atleast(pe, s_gelu, s + (p0 - 1))
                        for blk in range(2):
                            for k in range(KD):
                                ins = three(bank[:, 2 + par, blk * HR:(blk + 1) * HR],
                                            lambda h: XBT[h][:, par, k, blk, :],
                                            lambda h: expert(1, h, at[blk], k), k == 0, k == KD - 1)
                        ins.then_inc(s_mm1, 1)
                    if inside(s - 1, PAIRS):
                        at = before
                    if inside(s + 1, PAIRS):
                        load_experts(s + 1, 1 - par)
                    if inside(s - 1, PAIRS):
                        pe.wait_ge(s_hl, s + p0)
                        atleast(pe, s_yok, s + (p0 - 2))
                        for blk in range(2):
                            for k in range(KD):
                                ins = three(bank[:, 7 - par, blk * D:(blk + 1) * D],
                                            lambda h: HT[h][:, 1 - par, k, blk, :],
                                            lambda h: expert(2, h, at[blk], k), k == 0, k == KD - 1)
                        ins.then_inc(s_yps, 1)

                pe.wait_ge(s_table, layer + 1)
                offset = [[pe.alloc_register(f"expert_{layer}_{par}_{blk}") for blk in range(2)] for par in range(2)]
                run_steps(pe, step, -1, 4, PAIRS - 4, PAIRS + 1, 4)

            def attention_weights():
                pe.wait_ge(s_mat, 96)
                for i in range(3):
                    for m in range(KD):
                        for k in range(KD):
                            ins = pe.matmul(bank[:, 2 * i + m, 0:NW], raw_w[i][:, k, m * P:(m + 1) * P],
                                            raw_fwd[:, k, :], start=(k == 0), stop=(k == KD - 1))
                        ins.then_inc(s_mps, 1)

            def attention(s, par, half):
                def spectrum(i, to, done):
                    for r in range(2):
                        for k in range(KD):
                            ins = three(bank[:, to + r, :], lambda h: WF[h][:, k, i, r * NF:(r + 1) * NF],
                                        lambda h: XA[h][:, k, :], k == 0, k == KD - 1)
                    ins.then_inc(done, 1)

                now, nxt = inside(s, CH), inside(s + 1, CH)
                if now:
                    pe.wait_ge(s_nkv, s + 1)
                    pe.matmul(bank[:, 7, 32:32 + J], tri_f, ny[:, 64:64 + J], start=True, stop=False)
                    pe.matmul(bank[:, 7, 32:32 + J], ones_f, ny[:, 72:72 + J], start=False, stop=True).then_inc(s_nsum, 1)
                if nxt:
                    pe.wait_ge(s_txn, s + 2)
                    if isinstance(s, int) and s < 0:
                        pe.wait_ge(s_mlo, 3)
                    atleast(pe, s_aout, s * 2)
                    for k in range(KD):
                        for j in range(J):
                            ins = pe.transpose(bank[:, k, j * P:(j + 1) * P], XN[:, j, k * P:(k + 1) * P], ident)
                    ins.then_inc(s_atp, 1)
                    pe.wait_ge(s_al, s + 2)
                    atleast(pe, s_qev, s + 1)
                    spectrum(0, 2, s_kps)
                    atleast(pe, s_vused, s + 1)
                    spectrum(1, 4, s_vps)
                if now:
                    pe.wait_ge(s_npq, s + 1)
                    for j in range(J):
                        ins = pe.transpose(bank[0:1, 1, j * P:(j + 1) * P], ny[:, 80 + j:81 + j], ident)
                    ins.then_inc(s_nt, 1)
                if nxt:
                    for j in range(J):
                        for k in range(KD):
                            ins = three(bank[:, 7, j * 6:(j + 1) * 6].rearrange("p (a b) -> p a b", a=3),
                                        lambda h: XA[h][:, k, j * P:(j + 1) * P],
                                        lambda h: WF[h][:, k, :, D:NW], k == 0, k == KD - 1)
                    ins.then_inc(s_nps, 1)
                    pe.wait_ge(s_kev, s * 2 + 4)
                    spectrum(2, 2, s_qps)
                if now:
                    pe.wait_ge(s_pl, s + 1)
                    pe.wait_ge(s_nl, s + 1)
                    atleast(pe, s_aout, s * 2)
                    for half_ in range(2):
                        for i in range(2):
                            j = 2 * half_ + i
                            o = bank[:, 6 if half_ == 0 else 0, i * D:(i + 1) * D]
                            for r in range(2):
                                three(o, lambda h: VH[h][:, r, j * P:(j + 1) * P], lambda h: WI[h][:, r, :],
                                      r == 0, False)
                            pe.matmul(o, PN["h"][:, j, :], sign[:], start=False, stop=False)
                            ins = pe.matmul(o, PN["l"][:, j, :], sign[:], start=False, stop=True)
                        ins.then_inc(s_aps, 1)

            shared_weights(0)
            phase_a(0)
            pe.wait_ge(s_elo, 8)
            phase_b(0)
            attention_weights()
            run_steps(pe, attention, -1, 2, CH - 2, CH, 2)
            shared_weights(1)
            phase_a(1)
            phase_b(1)

        @block.vector
        def _(dve):
            ch = Tally(dve, s_dve)

            def low(o, v, h):
                return dve.tensor_tensor(o, v, h.bitcast(F32), ALU.subtract)

            def bc(a, n):
                return a.to_broadcast(n)

            def stats(c, par):
                for j in range(J):
                    ch.link(dve.bn_stats(st[:, par, j, :], X[:, bass.ds(c * J + j, 1), :].rearrange("p a d -> p (a d)")))
                ch.settle()
                apart(dve)
                for j in range(J):
                    ins = dve.bn_aggr(mv[:, par, j, :], st[:, par, j, :])
                ins.then_inc(s_var, 1)

            def shared_weights(layer):
                for i, w in enumerate((1, 3, 2)):
                    dve.wait_ge(s_whi, 4 * layer + i + 1)
                    low(SW[w, "l"][:], raw_sw[w][:], SW[w, "h"][:]).then_inc(s_wlo, 1)
                dve.wait_ge(s_whi, 4 * layer + 4)
                low(RW["l"][:], bank[:, 7, 0:KD * E].rearrange("p (k e) -> p k e", k=KD), RW["h"][:]).then_inc(s_wlo, 1)
                if layer == 0:
                    dve.wait_ge(s_rps, 2)
                    ch.link(dve.tensor_copy(bias_r[:].rearrange("p j e -> p (j e)"), bank[:, 6, 0:J * E]))

            def phase_a(layer):
                g0 = CH * layer
                flat = "p j e -> p (j e)"
                (sel, gt, eq, rk, msk, cnt, pick2, slotv, prod2) = (small[:, 0], small[:, 1], small[:, 2], small[:, 3],
                                                                    small[:, 4], small[:, 5], small[:, 6:8],
                                                                    small[:, 8], small[:, 9:11])
                m8, few = small[:, 11], small[:, 12].rearrange(flat)
                gsum = small[:, 13].rearrange(flat)
                res_e, res_j = cst[:, C_RESE:C_RESE + J * E], cst[:, C_RESJ:C_RESJ + J * E]

                def route(c):
                    g = c + g0
                    dve.wait_ge(s_prob, g + 1)
                    ch.link(dve.tensor_tensor(sel, prob[:], bias_r[:], ALU.add))
                    ch.settle()
                    apart(dve)
                    for j in range(J):
                        ch.link(dve.max(m8[:, j, :], sel[:, j, :]))
                    ch.settle()
                    second = bc(m8[:, :, 1:2], [P, J, E])
                    ch.link(dve.tensor_tensor(gt, sel, second, ALU.is_gt))
                    ch.link(dve.tensor_tensor(eq, sel, second, ALU.is_equal))
                    ch.settle()
                    ch.link(dve.tensor_reduce(few[:, 0:J], gt, AX.X, ALU.add))
                    ch.link(dve.tensor_tensor_scan(rk.rearrange(flat), res_e, eq.rearrange(flat), 0.0, ALU.mult, ALU.add))
                    ch.settle()
                    ch.link(dve.tensor_tensor(rk, rk, bc(few[:, 0:J].unsqueeze(2), [P, J, E]), ALU.add))
                    ch.settle()
                    ch.link(dve.scalar_tensor_tensor(eq, rk, float(TOPK), eq, ALU.is_le, ALU.mult))
                    ch.settle()
                    ch.link(dve.tensor_tensor(msk, gt, eq, ALU.add))
                    ch.settle()
                    ch.link(dve.tensor_copy(inc_b[:, 0].rearrange("p e j -> p j e"), msk))
                    ch.link(dve.tensor_copy(slotv.rearrange(flat).rearrange("p (e j) -> p j e", e=E), msk))
                    ch.link(dve.tensor_tensor_scan(cnt.rearrange(flat), res_e, msk.rearrange(flat), 0.0,
                                                   ALU.mult, ALU.add))
                    ch.settle()
                    dve.tensor_tensor_scan(inc_b[:, 1].rearrange("p e j -> p (e j)"), res_j,
                                           slotv.rearrange(flat), 0.0, ALU.mult, ALU.add).then_inc(s_mask, 1)

                def gate(c):
                    ch.settle()
                    for k in range(TOPK):
                        ch.link(dve.tensor_tensor(prod2[:, k], pick2[:, k], prob[:], ALU.mult))
                    ch.settle()
                    ch.link(dve.tensor_reduce(gsum[:, 0:2 * J].rearrange("p (k j) -> p k j", k=2), prod2, AX.X, ALU.add))
                    ch.settle()
                    ch.link(dve.tensor_tensor(gsum[:, 8:12], gsum[:, 0:J], gsum[:, J:2 * J], ALU.add))
                    ch.settle()
                    ch.link(dve.tensor_scalar(gsum[:, 12:16], gsum[:, 8:12], GATE_EPS, 0.5, ALU.is_gt, ALU.mult))
                    ch.link(dve.tensor_scalar(gsum[:, 16:20], gsum[:, 8:12], GATE_EPS, None, ALU.add))
                    ch.settle()
                    ch.link(dve.reciprocal(gsum[:, 16:20], gsum[:, 16:20]))
                    ch.link(dve.tensor_scalar(gsum[:, 20:24], gsum[:, 12:16], -1.0 / TOPK, 0.5 / TOPK,
                                              ALU.mult, ALU.add))
                    ch.settle()
                    ch.link(dve.tensor_tensor(gsum[:, 16:20], gsum[:, 16:20], gsum[:, 12:16], ALU.mult))
                    ch.settle()
                    for k in range(TOPK):
                        ch.link(dve.tensor_tensor(gsum[:, 4 * k:4 * k + 4], gsum[:, 4 * k:4 * k + 4], gsum[:, 16:20],
                                                  ALU.mult))
                    ch.settle()
                    for k in range(TOPK):
                        ins = dve.tensor_tensor(gates[:, k, bass.ds(c * J, J)], gsum[:, 4 * k:4 * k + 4],
                                                gsum[:, 20:24], ALU.add)
                        if k == 0:
                            ch.link(ins)
                    ins.then_inc(s_gated, 1)

                def places(c, par):
                    g = c + g0
                    ch.link(dve.scalar_tensor_tensor(pick2[:, 0], cnt, 1.0, msk, ALU.is_equal, ALU.mult))
                    ch.settle()
                    ch.link(dve.tensor_tensor(pick2[:, 1], msk, pick2[:, 0], ALU.subtract))
                    ch.settle()
                    dve.wait_ge(s_rank, g + 1)
                    ch.link(dve.tensor_tensor(slotv,
                                              bank[:, 7, 64:64 + J * E].rearrange("p (e j) -> p j e", e=E),
                                              bc(carry[:].unsqueeze(1), [P, J, E]), ALU.add))
                    ch.settle()
                    ch.link(dve.tensor_tensor(carry[:], carry[:], bank[:, 7, 128:128 + E], ALU.add))
                    for k in range(TOPK):
                        ch.link(dve.tensor_tensor(prod2[:, k], pick2[:, k], slotv, ALU.mult))
                    ch.settle()
                    ch.link(dve.tensor_reduce(few[:, 8:8 + 2 * J].rearrange("p (k j) -> p k j", k=2), prod2, AX.X, ALU.add))
                    ch.settle()
                    dve.tensor_copy(slots[:, par], few[:, 8:8 + 2 * J].rearrange("p (k j) -> p k j",
                                                                                 k=2)).then_inc(s_slot, 1)

                def hidden(s, m):
                    n = s * M + (g0 * M + m)
                    gu = gate_u[:, m % 2, :]
                    dve.wait_ge(s_sig, n + 1)
                    ch.link(dve.tensor_tensor(gu, gu, bank[:, 2 + 2 * (m % 2), :], ALU.mult))
                    ch.settle()
                    dve.tensor_tensor(gu, gu, bank[:, 3 + 2 * (m % 2), :], ALU.mult).then_inc(s_u, 1)

                def low_u(s, m):
                    n = s * M + (g0 * M + m)
                    dve.wait_ge(s_uh, n + 1)
                    low(U["l"][:, m, :], gate_u[:, m % 2, :], U["h"][:, m, :]).then_inc(s_ul, 1)

                def step(s, par, half):
                    now, nxt, far = inside(s, CH), inside(s + 1, CH), inside(s + 2, CH)
                    if inside(s - 1, CH):
                        for h in range(2):
                            dve.wait_ge(s_ops, s * 2 + (2 * g0 + h - 1))
                            xc = X[:, bass.ds(s * J + (2 * h - J), 2), :]
                            dve.scalar_tensor_tensor(xc, bank[:, 6 if h == 0 else 0, :].rearrange("p (j d) -> p j d", j=2),
                                                     0.5, xc, ALU.mult, ALU.add).then_inc(s_xout, 1)
                    if inside(s + 3, CH):
                        if layer == 0:
                            dve.wait_ge(s_x[1 - par], half * 16 + 32 + 16 * par)
                            apart(dve)
                        stats(s + 3, 1 - par)
                    if now:
                        low_u(s, 0)
                        low_u(s, 1)
                        hidden(s, 2)
                        low_u(s, 2)
                    if nxt:
                        route(s + 1)
                    if now:
                        hidden(s, 3)
                        low_u(s, 3)
                    if nxt:
                        hidden(s + 1, 0)
                        places(s + 1, 1 - par)
                        hidden(s + 1, 1)
                    if far:
                        dve.wait_ge(s_xh, s + (g0 + 3))
                        low(XT["l"][:, par], bank[:, 0:2, :], XT["h"][:, par]).then_inc(s_xl, 1)
                    if nxt:
                        gate(s + 1)

                dve.wait_ge(s_wlo, 4 * (layer + 1))
                dve.wait_ge(s_elo, 8)
                for par in range(2):
                    ch.link(dve.memset(rows[:, par, :, D:ROW], 0.0))
                ch.link(dve.tensor_copy(carry[:], cst[:, C_BASE:C_BASE + E]))
                ch.settle()
                run_steps(dve, step, -3, 2, CH - 4, CH + 1, 2, ch, DVE_A)

            def block_table(layer):
                one = slice(0, 1)
                n8, nb, cb = line[:, 0, 0:E], line[:, 1, 0:E], line[:, 2, 0:E]
                dve.wait_ge(s_gated, CH * (layer + 1))
                ch.settle()
                ch.link(dve.tensor_tensor(n8, carry[one, :], cst[one, C_BASE:C_BASE + E], ALU.subtract))
                ch.link(dve.tensor_copy(table[:, 2 * BLOCKS:2 * BLOCKS + E], carry[one, :]))
                ch.settle()
                ch.link(dve.tensor_tensor(over[:], bc(n8.unsqueeze(2), [1, E, TILES]),
                                          bc(cst[one, C_THR:C_THR + TILES].unsqueeze(1), [1, E, TILES]), ALU.is_gt))
                ch.settle()
                ch.link(dve.tensor_reduce(nb, over[:], AX.X, ALU.add))
                ch.settle()
                ch.link(dve.tensor_tensor_scan(cb, cst[one, C_ONE8:C_ONE8 + E], nb, 0.0, ALU.mult, ALU.add))
                ch.settle()
                blk = cst[one, C_BLK:C_BLK + BLOCKS]
                ch.link(dve.tensor_tensor(past[:, 0], bc(blk.unsqueeze(2), [1, BLOCKS, E]),
                                          bc(cb.unsqueeze(1), [1, BLOCKS, E]), ALU.is_ge))
                ch.settle()
                ch.link(dve.tensor_tensor(past[:, 1], past[:, 0], bc(nb.unsqueeze(1), [1, BLOCKS, E]), ALU.mult))
                ch.settle()
                ch.link(dve.tensor_reduce(line[:, 3:5], past[:], AX.X, ALU.add))
                ch.settle()
                ch.link(dve.tensor_tensor(line[:, 5], blk, line[:, 4], ALU.subtract))
                ch.link(dve.tensor_scalar(table[:, BLOCKS:2 * BLOCKS], line[:, 3], float(E - 1), None, ALU.min))
                ch.settle()
                ch.link(dve.tensor_scalar(line[:, 5], line[:, 5], float(P), None, ALU.mult))
                ch.settle()
                dve.scalar_tensor_tensor(table[:, 0:BLOCKS], line[:, 3], float(CAP), line[:, 5],
                                         ALU.mult, ALU.add).then_inc(s_table, 1)

            def phase_b(layer):
                p0 = PAIRS * layer

                def step(s, u, q):
                    par = u % 2
                    flat = "p k b t -> p (k b t)"
                    if inside(s - 1, PAIRS):
                        dve.wait_ge(s_hh, s + p0)
                        low(HT["l"][:, 1 - par].rearrange(flat), bank[:, 5 - par, :],
                            HT["h"][:, 1 - par].rearrange(flat)).then_inc(s_hl, 1)
                    if inside(s + 1, PAIRS):
                        slot = (u + 1) % 4
                        turn = q if u < 3 else q + 1
                        atleast(dve, s_ysc[slot], turn * 32 + YW * layer)
                        dve.wait_ge(s_bh, s + (p0 + 2))
                        dve.tensor_copy(goal[:, slot, :], XB[:, slot, :, D].bitcast(I32))
                        low(XBT["l"][:, 1 - par].rearrange(flat), bank[:, 1 - par, :],
                            XBT["h"][:, 1 - par].rearrange(flat)).then_inc(s_bl, 1)
                    if inside(s - 1, PAIRS):
                        slot = (u + 3) % 4
                        dve.wait_ge(s_yps, s + p0)
                        dve.tensor_copy(YB[:, slot].rearrange("p b d -> p (b d)"), bank[:, 7 - par, :]).then_inc(s_yok, 1)

                run_steps(dve, step, -1, 4, PAIRS - 4, PAIRS + 1, 4)

            def attention(s, par, half):
                now, nxt = inside(s, CH), inside(s + 1, CH)
                if nxt:
                    c = s + 1
                    dve.wait_ge(s_yg, c * 32 + 32)
                    for k in range(TOPK):
                        for j in range(J):
                            t = c * J + j
                            xt = X[:, bass.ds(t, 1), :].rearrange("p a d -> p (a d)")
                            ins = dve.scalar_tensor_tensor(xt, YG[:, k, j, :], gates[:, k, bass.ds(t, 1)], xt,
                                                           ALU.mult, ALU.add)
                            if k == 1 and j == J - 1:
                                ins.then_inc(s_comb, 1)
                            else:
                                ch.link(ins)
                        if k == 0:
                            ch.settle()
                    dve.wait_ge(s_comb, c + 1)
                    apart(dve)
                    stats(c, 1 - par)
                if inside(s - 1, CH):
                    dve.wait_ge(s_add, s)
                    for h in range(2):
                        dve.wait_ge(s_aps, s * 2 + (h - 1))
                        xc = X[:, bass.ds(s * J + (2 * h - J), 2), :]
                        dve.tensor_tensor(xc, xc, bank[:, 6 if h == 0 else 0, :].rearrange("p (j d) -> p j d", j=2),
                                          ALU.add).then_inc(s_aout, 1)
                if now:
                    dve.wait_ge(s_nps, s + 1)
                    nys, nya = ny[:, 0:24], ny[:, 24:48]
                    by = "p (j w) -> p j w"
                    ch.link(dve.tensor_copy(nys, bank[:, 7, 0:24]))
                    ch.settle()
                    ch.link(dve.scalar_tensor_tensor(nya, nys, -1.0, nys, ALU.mult, ALU.max))
                    if par == 0:
                        ch.link(dve.memset(ny[:, 72:73], 0.0))
                    else:
                        ch.link(dve.tensor_copy(ny[:, 72:73], ny[:, 76:77]))
                    ch.settle()
                    ch.link(dve.tensor_scalar(nya, nya, FFT_EPS, None, ALU.add))
                    ch.settle()
                    ch.link(dve.reciprocal(nya, nya))
                    ch.settle()
                    ch.link(dve.tensor_tensor(nya, nya, nys, ALU.mult))
                    ch.settle()
                    ch.link(dve.tensor_tensor(ny[:, 64:68], nya.rearrange(by, w=6)[:, :, 0],
                                              nys.rearrange(by, w=6)[:, :, 2], ALU.mult))
                    ch.settle()
                    dve.tensor_tensor_scan(ny[:, 73:77], cst[:, C_ONE8:C_ONE8 + J], ny[:, 64:68], ny[:, 72:73],
                                           ALU.mult, ALU.add).then_inc(s_nkv, 1)
                    dve.wait_ge(s_kroot, s + 1)
                    ch.link(dve.tensor_scalar(RN[:, 0, :], RN[:, 0, :], FFT_EPS, None, ALU.add))
                    ch.settle()
                    ch.link(dve.reciprocal(RN[:, 0, :], RN[:, 0, :]))
                    ch.settle()
                    ch.link(dve.tensor_tensor(FK[:], FK[:], bc(RN[:, 0:1, :], [P, 2, N]), ALU.mult))
                    if par == 1:
                        ch.link(dve.tensor_copy(ny[:, 48:50], CUM[:, :, N - 1]))
                    ch.settle()
                if nxt:
                    dve.wait_ge(s_ah, s + 2)
                    low(XA["l"][:], bank[:, 0:2, :], XA["h"][:]).then_inc(s_al, 1)
                if now:
                    dve.wait_ge(s_qroot, s + 1)
                    ch.link(dve.tensor_scalar(RN[:, 1, :], RN[:, 1, :], FFT_EPS, None, ALU.add))
                    ch.settle()
                    dve.reciprocal(RN[:, 1, :], RN[:, 1, :]).then_inc(s_qinv, 1)
                    dve.wait_ge(s_vps, s + 1)
                    ch.link(dve.tensor_tensor(PR[:], FK[:], bank[:, 4:6, :], ALU.mult))
                    ch.settle()
                    ch.link(dve.tensor_tensor_scan(CUM[:, 0, :], PR[:, 0, :], PR[:, 1, :],
                                                   ny[:, 48:49] if par == 1 else 0.0, ALU.add, ALU.subtract))
                    ch.settle()
                    ch.link(dve.tensor_tensor(PR[:, 0, :], FK[:, 1, :], bank[:, 4, :], ALU.mult))
                    dve.tensor_tensor(PR[:, 1, :], FK[:, 0, :], bank[:, 5, :], ALU.mult).then_inc(s_vused, 1)
                    dve.wait_ge(s_vused, s + 1)
                    dve.tensor_tensor_scan(CUM[:, 1, :], PR[:, 0, :], PR[:, 1, :],
                                           ny[:, 49:50] if par == 1 else 0.0, ALU.add, ALU.add).then_inc(s_kvd, 1)
                    dve.wait_ge(s_nsum, s + 1)
                    dve.tensor_tensor(ny[:, 80:84], bank[:, 7, 32:36], nya.rearrange(by, w=6)[:, :, 4],
                                      ALU.mult).then_inc(s_npq, 1)
                    dve.wait_ge(s_kvd, s + 1)
                    dve.wait_ge(s_qn, s + 1)
                    ch.link(dve.tensor_tensor(PQ[:], CUM[:], FQ[:], ALU.mult))
                    ch.link(dve.tensor_tensor(PS[:, 0, :], CUM[:, 1, :], FQ[:, 0, :], ALU.mult))
                    ch.settle()
                    dve.wait_ge(s_ps, s + 1)
                    ch.link(dve.tensor_tensor(KV[:, 0, :], PQ[:, 0, :], PQ[:, 1, :], ALU.add))
                    ch.settle()
                    dve.tensor_tensor(KV[:, 1, :], PS[:, 0, :], PS[:, 1, :], ALU.subtract).then_inc(s_p, 1)
                    dve.wait_ge(s_nh, s + 1)
                    low(PN["l"][:].rearrange("p j t -> p (j t)"), bank[0:1, 1, :],
                        PN["h"][:].rearrange("p j t -> p (j t)")).then_inc(s_nl, 1)
                    dve.wait_ge(s_ph, s + 1)
                    low(VH["l"][:], KV[:], VH["h"][:]).then_inc(s_pl, 1)

            dve.wait_ge(s_const, 32)
            ch.link(dve.tensor_copy(ones_b[:], ones_f))
            ch.link(dve.scalar_tensor_tensor(tri_b[:], tri_f, 1.0, ident, ALU.subtract, ALU.subtract))
            ch.link(dve.memset(neg_one[:], -1.0))
            ch.settle()
            dve.memset(half_neg[:], -0.5).then_inc(s_small, 1)
            shared_weights(0)
            for w in (1, 2):
                raw = raw_ew[w][:].rearrange("p e k n -> p (e k n)")
                for n, i in enumerate(range(0, E * KD * HR, 1024)):
                    dve.wait_ge(s_ehi, 4 * (w - 1) + n + 1)
                    low(EW[w, "l"][:, i:i + 1024], raw[:, i:i + 1024], EW[w, "h"][:, i:i + 1024]).then_inc(s_elo, 1)
            phase_a(0)
            block_table(0)
            phase_b(0)
            dve.wait_ge(s_mhi, 2)
            low(WI["l"][:], raw_inv[:], WI["h"][:]).then_inc(s_mlo, 1)
            for i in range(3):
                for k in range(KD):
                    dve.wait_ge(s_mhi, 2 * i + k + 3)
                    ch.link(low(WF["l"][:, k, i, :], bank[:, 2 * i + k, 0:NW], WF["h"][:, k, i, :]))
            ch.settle()
            dve.nop().then_inc(s_mlo, 2)
            run_steps(dve, attention, -1, 2, CH - 2, CH + 1, 2, ch, DVE_T)
            dve.wait_ge(s_aout, 2 * CH)
            shared_weights(1)
            phase_a(1)
            block_table(1)
            phase_b(1)

            def last(c, slot, q):
                dve.wait_ge(s_f[slot], q * 32 + 32)
                for k in range(TOPK):
                    for j in range(J):
                        t = c * J + j
                        xt = X[:, bass.ds(t, 1), :].rearrange("p a d -> p (a d)")
                        ins = dve.scalar_tensor_tensor(xt, YF[:, slot, k, j, :], gates[:, k, bass.ds(t, 1)], xt,
                                                       ALU.mult, ALU.add)
                        if k == 1 and j == J - 1:
                            ins.then_inc(s_fc, 1)
                        else:
                            ch.link(ins)
                    if k == 0:
                        ch.settle()

            dve.wait_ge(s_xout, 4 * CH)
            run_steps(dve, last, 0, 4, CH, CH, 4, ch, 28)


_INS = ["L0_attn_x", "L0_attn_Wq", "L0_attn_Wk", "L0_attn_Wv", "L0_ffn_router_w", "L0_ffn_router_bias", "L0_ffn_sw1",
        "L0_ffn_sw3", "L0_ffn_sw2", "L0_ffn_ew1", "L0_ffn_ew2"]


def kernel(**inputs):
    import concourse.bacc as bacc
    from concourse.bass_utils import run_bass_kernel_spmd

    nc = bacc.Bacc("TRN2", target_bir_lowering=False, num_devices=1)
    data = {f"in_{n}": np.ascontiguousarray(inputs[n]) for n in _INS}
    data.update({f"in_{n}": a for n, a in constants().items()})
    args = {n: nc.dram_tensor(n, a.shape, mybir.dt.from_np(a.dtype), kind="ExternalInput").ap() for n, a in data.items()}
    out = nc.dram_tensor("out_0", (B, S, D), F32, kind="ExternalOutput").ap()
    build(nc, *(args[f"in_{n}"] for n in _INS), args["in_c_main"], args["in_c_fwd"], args["in_c_inv"], args["in_c_tok"],
          args["in_c_fill"], args["in_c_sign"], out)
    return run_bass_kernel_spmd(nc, [data], core_ids=[0]).results[0]["out_0"]
```
